# Optimizing a Trainium2 kernel written in Bass

```python
import numpy as np
import jax
import jax.numpy as jnp

def _softmax(x, axis=-1):
    return jax.nn.softmax(x, axis=axis)

def _gelu(x):
    return jax.nn.gelu(x, approximate=True)

def _silu(x):
    return jax.nn.silu(x)

def _sigmoid(x):
    return jax.nn.sigmoid(x)

def _layernorm(x, axis=-1, eps=1e-05):
    m = jnp.mean(x, axis=axis, keepdims=True)
    v = jnp.var(x, axis=axis, keepdims=True)
    return (x - m) / jnp.sqrt(v + eps)

def _scatter_add(tgt, idx, src, axis=0):
    return tgt.at[idx].add(src)

def _segment_sum(src, seg, n):
    return jax.ops.segment_sum(src, seg, n)
kernel_name = 'mk_gps_d1_gnn_r8_8bc92b'

def setup_inputs(seed: int=0):
    np.random.seed(seed)
    _w = jnp.asarray

    def _rec_inputs():
        import jax
        import jax.numpy as jnp
        _gk = jax.random.key(seed)
        x = -0.0006008 + 1.001 * jax.random.normal(jax.random.fold_in(_gk, 1), (6250, 256), jnp.float32)
        src = jax.random.randint(jax.random.fold_in(_gk, 2), (200000,), 0, 6250, jnp.int32)
        dst = jax.random.randint(jax.random.fold_in(_gk, 3), (200000,), 0, 6250, jnp.int32)
        _o = jnp.argsort(dst, stable=True)
        src = src[_o]
        dst = dst[_o]
        return (x, src, dst)
    x, src, dst = _rec_inputs()

    def _L0_gnn_setup():
        import jax, jax.numpy as jnp
        import numpy as np
        N_NODES = 1250
        N_EDGES = 40000
        D_IN = 256
        D_OUT = 256
        key = jax.random.key(seed)
        k1, k2, k3, k4 = jax.random.split(key, 4)
        x = jax.random.normal(k1, (N_NODES, D_IN), dtype=jnp.float32)
        edge_index = jax.random.randint(k2, (2, N_EDGES), 0, N_NODES, dtype=jnp.int64)
        weight = jax.random.normal(k3, (2 * D_IN, D_OUT), dtype=jnp.float32) / np.sqrt(2 * D_IN)
        bias = jax.random.normal(k4, (D_OUT,), dtype=jnp.float32)
        return {'x': x, 'edge_index': edge_index, 'weight': weight, 'bias': bias}
    _L0_gnn_all = _L0_gnn_setup()
    _L0_gnn_in = {k: v for k, v in _L0_gnn_all.items() if k in ('weight', 'bias')}
    del _L0_gnn_all

    def _L0_mix_setup():
        import jax, jax.numpy as jnp
        import numpy as np
        A, Bc, Cc = (0.5, 1.0, 1.0)
        H = 8
        EPS = 1e-12

        def _normalize(t):
            n = jnp.linalg.norm(t, axis=-1, keepdims=True)
            return t / jnp.maximum(n, EPS)
        key = jax.random.key(seed)
        ks = jax.random.split(key, 5)
        B, N, C = (8, 256, 256)
        D = C // H
        x = jax.random.normal(ks[0], (B, N, C), dtype=jnp.float32)
        Wqkv = jax.random.normal(ks[1], (3 * H * D, C), dtype=jnp.float32) * 0.02
        bqkv = jnp.zeros((3 * H * D,), dtype=jnp.float32)
        Wproj = jax.random.normal(ks[2], (C, H * D), dtype=jnp.float32) * 0.02
        bproj = jnp.zeros((C,), dtype=jnp.float32)
        temperature = jnp.ones((1, H, 1, 1), dtype=jnp.float32)
        return {'x': x, 'Wqkv': Wqkv, 'bqkv': bqkv, 'Wproj': Wproj, 'bproj': bproj, 'temperature': temperature}
    _L0_mix_all = _L0_mix_setup()
    _L0_mix_in = {k: v for k, v in _L0_mix_all.items() if k in ('Wqkv', 'bqkv', 'Wproj', 'bproj', 'temperature')}
    del _L0_mix_all

    def _L0_ffn_setup():
        import jax, jax.numpy as jnp
        import numpy as np
        B, S, D, E, H, K = (4, 512, 256, 8, 512, 2)
        key = jax.random.key(seed)
        ks = jax.random.split(key, 6)
        x = jax.random.normal(ks[0], (B, S, D), jnp.float32)
        Wg = jax.random.normal(ks[1], (D, E), jnp.float32) * 0.02
        bg = jnp.zeros((E,), jnp.float32)
        W1 = jax.random.normal(ks[2], (E, D, H), jnp.float32) * 0.02
        b1 = jnp.zeros((E, H), jnp.float32)
        W2 = jax.random.normal(ks[3], (E, H, D), jnp.float32) * 0.02
        b2 = jnp.zeros((E, D), jnp.float32)
        return {'x': x, 'Wg': Wg, 'bg': bg, 'W1': W1, 'b1': b1, 'W2': W2, 'b2': b2}
    _L0_ffn_all = _L0_ffn_setup()
    _L0_ffn_in = {k: v for k, v in _L0_ffn_all.items() if k in ('Wg', 'bg', 'W1', 'b1', 'W2', 'b2')}
    del _L0_ffn_all
    return {'x': x, 'src': src, 'dst': dst, 'L0_gnn_weight': _L0_gnn_in['weight'], 'L0_gnn_bias': _L0_gnn_in['bias'], 'L0_mix_Wqkv': _L0_mix_in['Wqkv'], 'L0_mix_bqkv': _L0_mix_in['bqkv'], 'L0_mix_Wproj': _L0_mix_in['Wproj'], 'L0_mix_bproj': _L0_mix_in['bproj'], 'L0_mix_temperature': _L0_mix_in['temperature'], 'L0_ffn_Wg': _L0_ffn_in['Wg'], 'L0_ffn_bg': _L0_ffn_in['bg'], 'L0_ffn_W1': _L0_ffn_in['W1'], 'L0_ffn_b1': _L0_ffn_in['b1'], 'L0_ffn_W2': _L0_ffn_in['W2'], 'L0_ffn_b2': _L0_ffn_in['b2']}

def reference(x, src, dst, L0_gnn_weight, L0_gnn_bias, L0_mix_Wqkv, L0_mix_bqkv, L0_mix_Wproj, L0_mix_bproj, L0_mix_temperature, L0_ffn_Wg, L0_ffn_bg, L0_ffn_W1, L0_ffn_b1, L0_ffn_W2, L0_ffn_b2):
    import jax
    import jax.numpy as jnp

    def _L0_gnn_ref(x, edge_index, weight, bias):
        import jax, jax.numpy as jnp
        import numpy as np
        N_NODES = 1250
        N_EDGES = 40000
        D_IN = 256
        D_OUT = 256
        n = x.shape[0]
        src, dst = (edge_index[0], edge_index[1])
        summed = jax.ops.segment_sum(x[src], dst, num_segments=n)
        deg = jax.ops.segment_sum(jnp.ones_like(src, dtype=x.dtype), dst, num_segments=n)
        agg = summed / jnp.maximum(deg, 1.0)[:, None]
        out = jnp.concatenate([x, agg], axis=-1) @ weight
        out = out / jnp.linalg.norm(out, axis=-1, keepdims=True)
        return out + bias

    def _L0_mix_ref(x, Wqkv, bqkv, Wproj, bproj, temperature):
        import jax, jax.numpy as jnp
        import numpy as np
        A, Bc, Cc = (0.5, 1.0, 1.0)
        H = 8
        EPS = 1e-12

        def _normalize(t):
            n = jnp.linalg.norm(t, axis=-1, keepdims=True)
            return t / jnp.maximum(n, EPS)
        B, N, C = x.shape
        D = C // H
        scale = float(D) ** 0.25
        qkv = (x @ Wqkv.T + bqkv).reshape(B, N, 3, H, D)
        qkv = jnp.transpose(qkv, (2, 0, 3, 1, 4))
        q, k, v = (qkv[0], qkv[1], qkv[2])
        q = q * scale
        v1 = jnp.concatenate([jnp.ones((B, H, N, 1), dtype=v.dtype), v], axis=-1)
        qn = _normalize(q) * (scale * temperature)
        kn = _normalize(k) * scale
        vN = v1 / N
        kv_mod = jnp.einsum('bhni,bhnj,bhne->bhije', kn, kn, vN)
        kv = jnp.einsum('bhnd,bhne->bhde', kn, vN)
        vsum = jnp.sum(vN, axis=-2)[:, :, None, :]
        y = A * jnp.einsum('bhni,bhnj,bhije->bhne', qn, qn, kv_mod) + scale ** 2 * Bc * jnp.einsum('bhnd,bhde->bhne', qn, kv) + scale ** 4 * Cc * vsum
        y_norm, y = (y[..., :1], y[..., 1:])
        y = y / y_norm
        out = jnp.transpose(y, (0, 2, 1, 3)).reshape(B, N, H * D)
        return out @ Wproj.T + bproj

    def _L0_ffn_ref(x, Wg, bg, W1, b1, W2, b2):
        import jax, jax.numpy as jnp
        import numpy as np
        B, S, D, E, H, K = (4, 512, 256, 8, 512, 2)
        Bv, Sv, Dv = x.shape
        gate_scores = x @ Wg + bg
        _, idx = jax.lax.top_k(gate_scores, K)
        mask = jax.nn.one_hot(idx, E, dtype=x.dtype).sum(axis=-2)
        xf = x.reshape(-1, Dv)
        mf = mask.reshape(-1, E)
        h = jax.nn.gelu(jnp.einsum('td,edh->teh', xf, W1) + b1[None], approximate=False)
        y = jnp.einsum('teh,ehd->ted', h, W2) + b2[None]
        out = jnp.einsum('ted,te->td', y, mf)
        return out.reshape(Bv, Sv, Dv)
    edge_index = jnp.stack([src, dst])
    xn = _layernorm(x, axis=-1)
    x = x + _L0_gnn_ref(xn, edge_index, L0_gnn_weight, L0_gnn_bias) + _L0_mix_ref(xn[None], L0_mix_Wqkv, L0_mix_bqkv, L0_mix_Wproj, L0_mix_bproj, L0_mix_temperature)[0]
    x = x + _L0_ffn_ref(_layernorm(x, axis=-1)[None], L0_ffn_Wg, L0_ffn_bg, L0_ffn_W1, L0_ffn_b1, L0_ffn_W2, L0_ffn_b2)[0]
    return x

_drawn_inputs = setup_inputs


def setup_inputs(seed=0):
    import zlib

    import numpy as np

    out = dict(_drawn_inputs(seed))
    spreads = {'L0_mix_bqkv': (0.0, 0.1),
     'L0_mix_bproj': (0.0, 0.1),
     'L0_mix_temperature': (1.0, 0.6),
     'L0_ffn_bg': (0.0, 0.1),
     'L0_ffn_b1': (0.0, 0.312),
     'L0_ffn_b2': (0.0, 0.1)}
    factors = {'L0_mix_Wqkv': 22.625}
    for name, (base, spread) in spreads.items():
        noise = np.random.default_rng([zlib.crc32(name.encode()), seed]).standard_normal(out[name].shape)
        drawn = base * np.exp(spread * noise) if base else spread * noise
        out[name] = jnp.asarray(drawn.astype(out[name].dtype))
    for name, factor in factors.items():
        out[name] = (out[name] * factor).astype(out[name].dtype)
    return out
```

```python
from contextlib import ExitStack

import numpy as np

import concourse.bass as bass
from concourse import mybir
from concourse.bass import AP

F32 = mybir.dt.float32
BF16 = mybir.dt.bfloat16
I32 = mybir.dt.int32
U32 = mybir.dt.uint32
ALU = mybir.AluOpType
ACT = mybir.ActivationFunctionType
X = mybir.AxisListType.X

P = 128
N, D, E = 6250, 256, 200000
H, HD = 8, 32
TILES = -(-N // P)
LAST = N - (TILES - 1) * P
PAIRS = (TILES - 1) // 2
CH = 8
BATCHES = -(-E // (CH * P))
SLOTS = 4
ROW = 3 * D + 2
SUMS = D + 1
EXT = HD + 16
QUAD = 16 * HD
TAIL = HD + 16 + 1
NX, FF = 8, 512
CAP = 51 * P
UNIT = 2 * P
UNITS = (2 * N + NX * UNIT) // UNIT + 1
CODE = 64
SCALE = float(HD) ** 0.25
LN_EPS = 1e-5
NORM_EPS = 1e-12

C_EYE, C_UP, C_IOTA, C_WIN = 0, P, 2 * P, 3 * P
C_QUAD = C_WIN + TILES
C_LIN, C_ONE = C_QUAD + 5, C_QUAD + 10
C_E, C_BASE = C_QUAD + 15, C_QUAD + 15 + NX
C_ALL = C_BASE + NX


def constants():
    c = np.zeros((P, C_ALL), np.float32)
    c[:, C_EYE:C_EYE + P] = np.eye(P)
    c[:, C_UP:C_UP + P] = np.triu(np.ones((P, P)), 1)
    c[:, C_IOTA:C_IOTA + P] = np.arange(P)
    c[:, C_WIN:C_WIN + TILES] = P * np.arange(TILES)
    f = SCALE ** 4 / N
    c[:, C_QUAD:C_QUAD + 4] = f
    c[0:HD, C_QUAD] = 0.5 * f
    c[HD:HD + 16, C_QUAD + 4] = f
    c[0:HD, C_LIN + 4] = f
    c[HD + 16, C_ONE + 4] = f
    c[:, C_E:C_E + NX] = np.arange(NX)
    c[:, C_BASE:C_BASE + NX] = CAP * np.arange(NX)
    return c


def wait(e, sem, value):
    if not isinstance(value, int) or value > 0:
        e.wait_ge(sem, value)


def hold(pool, scratch, held, before):
    pool.wait_ge(held, before + 1)
    pool.tensor_tensor(scratch[0:1, 1:2], scratch[0:1, 0:1], scratch[0:1, 0:1], ALU.add).then_inc(held, 1)


def rows_of(dram, tile, rows, width):
    return dram[bass.ds(tile * P, rows), 0:width]


def window(nc, e, value):
    return nc.s_assert_within(e.snap(value), 0, TILES - 1,
                              skip_runtime_bounds_check_because="edges end at nodes, and nodes are in windows below TILES")


def windows_of(nc, e, win, pair):
    code = e.value_load(win[0:1, bass.ds(pair, 1)], min_val=0, max_val=CODE ** 4 - 1)
    digit = lambda i: window(nc, e, (code >> (6 * i)) & (CODE - 1))
    return (digit(0), digit(1)), (digit(2), digit(3))


def tile_loop(e, body):
    for u in range(2):
        body(0, u, u, P)
    with e.Fori(1, PAIRS) as turn:
        for u in range(2):
            body(turn, u, turn * 2 + u, P)
    body(PAIRS, 0, TILES - 1, LAST)


def four_tile_loop(e, body):
    for u in range(4):
        body(0, u, u, P)
    with e.Fori(1, TILES // 4) as turn:
        for u in range(4):
            body(turn, u, turn * 4 + u, P)
    body(TILES // 4, 0, TILES - 1, LAST)


def build(nc, A):
    dram = lambda name, shape, dt: nc.dram_tensor(name, shape, dt, kind="Internal").ap()
    d_xn = dram("d_xn", [TILES * P, D], F32)
    d_table = dram("d_table", [N + 1, ROW], BF16)
    d_win = dram("d_win", [BATCHES // 2, 1], I32)
    d_q = dram("d_q", [TILES * P, H * EXT], F32)
    d_xt = dram("d_xt", [TILES * P, D], F32)
    d_mix = dram("d_mix", [TILES * P, D], F32)
    d_x1 = dram("d_x1", [TILES * P, D], F32)
    d_slot = dram("d_slot", [NX * CAP, D], F32)
    d_y = dram("d_y", [UNITS * UNIT, D], F32)

    with ExitStack() as whole:
        ws = lambda name, shape, dt: whole.enter_context(nc.sbuf_tensor(name, shape, dt))
        cst = ws("cst", [P, C_ALL], F32)
        win = ws("win", [1, BATCHES // 2], I32)
        agg = ws("agg", [P, TILES, SUMS], F32)
        pos = ws("pos", [P, TILES + 3, 2], I32)
        units = ws("units", [1, NX], I32)
        ends = ws("ends", [1, NX], I32)
        norm_stage(nc, A, cst, win, agg, d_xn, d_table, d_win)
        mix_stage(nc, A, cst, win, agg, d_xn, d_table, d_q, d_xt, d_mix)
        node_stage(nc, A, cst, agg, pos, units, ends, d_xt, d_mix, d_x1, d_slot)
        expert_stage(nc, A, cst, units, d_slot, d_y)
        combine_stage(nc, A, pos, d_x1, d_y)


def norm_stage(nc, A, cst, win, agg, d_xn, d_table, d_win):
    G = 4
    GROUPS = (TILES - 1) // G
    HALF = BATCHES // 2
    with ExitStack() as ctx:
        sb = lambda name, shape, dt: ctx.enter_context(nc.sbuf_tensor(name, shape, dt))
        sem = lambda name: ctx.enter_context(nc.semaphore(name))
        xg = [sb(f"n_x{u}", [P, G, D], F32) for u in range(2)]
        xn = [sb(f"n_xn{u}", [P, G, D], F32) for u in range(2)]
        rest = [sb(f"n_rest{u}", [P, G, D], F32) for u in range(2)]
        tab = [sb(f"n_tab{u}", [P, G, ROW], BF16) for u in range(2)]
        stats = sb("n_stats", [P, G, 6], F32)
        mv = sb("n_mv", [P, G, 2], F32)
        std = sb("n_std", [P, G], F32)
        rstd = sb("n_rstd", [P, G], F32)
        eps = sb("n_eps", [P, 1], F32)
        held = sb("n_held", [1, 1], F32)
        zero = sb("n_zero", [1, ROW], BF16)
        dst = sb("n_dst", [HALF, 2, CH * P], I32)
        ext = sb("n_ext", [HALF, 2, 2], I32)
        shifted = sb("n_shift", [HALF, 2, 2], I32)
        extra = sb("n_extra", [HALF, 2], I32)
        extra64 = sb("n_extra64", [HALF, 2], I32)
        code = sb("n_code", [HALF, 2], I32)
        code2 = sb("n_code2", [HALF, 1], I32)
        codes = sb("n_codes", [HALF, 1], I32)

        x_in = [sem(f"n_x_in{u}") for u in range(2)]
        table_out = [sem(f"n_table_out{u}") for u in range(2)]
        xn_out = [sem(f"n_xn_out{u}") for u in range(2)]
        cst_in, dst_in, zero_out = sem("n_cst_in"), sem("n_dst_in"), sem("n_zero_out")
        win_moved = sem("n_win_moved")
        ready = sem("n_ready")
        dve = sem("n_dve")
        var_ready, std_ready = sem("n_var_ready"), sem("n_std_ready")
        xn_ready, high_ready = sem("n_xn_ready"), sem("n_high_ready")
        rest_ready, mid_ready = sem("n_rest_ready"), sem("n_mid_ready")
        low_ready, agg_cleared = sem("n_low_ready"), sem("n_agg_cleared")
        codes_ready, stats_ready, rstd_ready = sem("n_codes_ready"), sem("n_stats_ready"), sem("n_rstd_ready")

        def groups(e, body):
            for u in range(2):
                body(0, u, u, G, P)
            with e.Fori(1, GROUPS // 2) as turn:
                for u in range(2):
                    body(turn, u, turn * 2 + u, G, P)
            body(GROUPS // 2, 0, GROUPS, 1, LAST)

        def node_rows(dram, g, n, rows):
            if n == 1:
                return dram[bass.ds(g * G * P, rows), :]
            return dram[bass.ds(g * G * P, G * P), :].rearrange("(j p) c -> p j c", p=P)

        def tiles_of(buf, n, rows):
            return buf[0:rows, 0, :] if n == 1 else buf[:, :, :]

        with nc.Block() as block:

            @block.sync
            def _(e):
                e.dma_start(cst[:, :], A["cst"]).then_inc(cst_in, 16)
                e.dma_start(dst[:, :, :], A["dst_rows"].rearrange("p (j c) -> p j c", j=2)).then_inc(dst_in, 16)

                def load(turn, u, g, n, rows):
                    wait(e, xn_ready, g - 1)
                    e.dma_start(tiles_of(xg[u], n, P), node_rows(A["x"], g, n, P)).then_inc(x_in[u], 16)

                groups(e, load)
                e.wait_ge(codes_ready, 1)
                e.dma_start(d_win[:, :], codes[:, :]).then_inc(win_moved, 16)
                e.wait_ge(win_moved, 16)
                e.dma_start(win[0:1, :], d_win.rearrange("(o p) c -> o (p c)", o=1)).then_inc(win_moved, 16)
                e.wait_ge(win_moved, 32)
                e.wait_ge(cst_in, 16)

            @block.gpsimd
            def _(e):
                def store(turn, u, g, n, rows):
                    e.wait_ge(xn_ready, g + 1)
                    e.dma_start(node_rows(d_xn, g, n, P), tiles_of(xn[u], n, P)).then_inc(xn_out[u], 16)
                    e.wait_ge(low_ready, g + 1)
                    e.wait_ge(mid_ready, g + 1)
                    e.dma_start(node_rows(d_table, g, n, rows), tiles_of(tab[u], n, rows)).then_inc(table_out[u], 16)

                e.memset(agg[:, :, :], 0.0).then_inc(agg_cleared, 1)
                e.wait_ge(agg_cleared, 1)
                e.wait_ge(ready, 1)
                e.dma_start(d_table[N:N + 1, :], zero[0:1, :]).then_inc(zero_out, 16)
                groups(e, store)
                for u, uses in ((0, GROUPS // 2 + 1), (1, GROUPS // 2)):
                    e.wait_ge(xn_out[u], 16 * uses)
                    e.wait_ge(table_out[u], 16 * uses)
                e.wait_ge(zero_out, 16)

            @block.scalar
            def _(e):
                e.wait_ge(ready, 1)

                def parts(turn, u, g, n, rows):
                    e.wait_ge(var_ready, g + 1)
                    e.activation(std[:, 0:n], mv[:, 0:n, 1], ACT.Sqrt, bias=eps[:, 0:1]).then_inc(std_ready, 1)
                    e.wait_ge(xn_ready, g + 1)
                    wait(e, table_out[u], turn * 16)
                    e.activation(tab[u][:, 0:n, 0:D], xn[u][:, 0:n, :], ACT.Copy).then_inc(high_ready, 1)
                    e.wait_ge(rest_ready, g + 1)
                    e.activation(tab[u][:, 0:n, D:2 * D], rest[u][:, 0:n, :], ACT.Copy).then_inc(mid_ready, 1)

                groups(e, parts)

            @block.vector
            def _(e):
                e.memset(eps[:, :], LN_EPS)
                e.memset(zero[:, :], 0.0)
                for u in range(2):
                    e.memset(tab[u][:, :, 3 * D:3 * D + 1], 1.0)
                    e.memset(tab[u][:, :, 3 * D + 1:ROW], 0.0)
                e.drain().then_inc(ready, 1)

                e.wait_ge(dst_in, 16)
                e.tensor_reduce(ext[:, :, 0], dst[:, :, :], X, ALU.min)
                e.tensor_reduce(ext[:, :, 1], dst[:, :, :], X, ALU.max).then_inc(dve, 1)
                e.wait_ge(dve, 1)
                e.tensor_scalar(shifted[:, :, :], ext[:, :, :], 7, None, ALU.arith_shift_right).then_inc(dve, 1)
                e.wait_ge(dve, 2)
                e.tensor_tensor(extra[:, :], shifted[:, :, 1], shifted[:, :, 0], ALU.subtract).then_inc(dve, 1)
                e.wait_ge(dve, 3)
                e.tensor_scalar(extra64[:, :], extra[:, :], float(CODE), None, ALU.mult).then_inc(dve, 1)
                e.wait_ge(dve, 4)
                e.tensor_tensor(code[:, :], extra64[:, :], shifted[:, :, 0], ALU.add).then_inc(dve, 1)
                e.wait_ge(dve, 5)
                e.tensor_scalar(code2[:, :], code[:, 1:2], float(CODE * CODE), None, ALU.mult).then_inc(dve, 1)
                e.wait_ge(dve, 6)
                e.tensor_tensor(codes[:, :], code2[:, :], code[:, 0:1], ALU.add).then_inc(codes_ready, 1)

                def statistics(g, u, count, n):
                    e.wait_ge(x_in[u], count)
                    for j in range(n):
                        last = e.bn_stats(stats[:, j, :], xg[u][:, j, :])
                    last.then_inc(stats_ready, 1)
                    e.wait_ge(stats_ready, g + 1)
                    wait(e, xn_ready, g)
                    e.memset(held[:, :], 0.0)
                    for j in range(n):
                        last = e.bn_aggr(mv[:, j, :], stats[:, j, :])
                    last.then_inc(var_ready, 1)

                def rows_norm(turn, u, g, n, rows):
                    e.wait_ge(std_ready, g + 1)
                    e.reciprocal(rstd[:, 0:n], std[:, 0:n]).then_inc(rstd_ready, 1)
                    e.wait_ge(rstd_ready, g + 1)
                    wait(e, xn_out[u], turn * 16)
                    for j in range(n):
                        last = e.tensor_scalar(xn[u][:, j, :], xg[u][:, j, :], mv[:, j, 0:1],
                                               rstd[:, j:j + 1], ALU.subtract, ALU.mult)
                    last.then_inc(xn_ready, 1)
                    if n > 1:
                        statistics(g + 1, 1 - u, (turn + u) * 16 + 16, G)
                    e.wait_ge(high_ready, g + 1)
                    e.tensor_tensor(rest[u][:, 0:n, :], xn[u][:, 0:n, :], tab[u][:, 0:n, 0:D],
                                    ALU.subtract).then_inc(rest_ready, 1)
                    e.wait_ge(mid_ready, g + 1)
                    e.tensor_tensor(tab[u][:, 0:n, 2 * D:3 * D], rest[u][:, 0:n, :],
                                    tab[u][:, 0:n, D:2 * D], ALU.subtract).then_inc(low_ready, 1)

                statistics(0, 0, 16, G)
                groups(e, rows_norm)


def mix_stage(nc, A, cst, win, agg, d_xn, d_table, d_q, d_xt, d_mix):
    with ExitStack() as ctx:
        sb = lambda name, shape, dt: ctx.enter_context(nc.sbuf_tensor(name, shape, dt))
        sem = lambda name: ctx.enter_context(nc.semaphore(name))
        two = lambda name: [sem(f"{name}{u}") for u in range(2)]
        ring = [sb(f"m_ring{s}", [P, CH, ROW], BF16) for s in range(SLOTS)]
        idx = [sb(f"m_idx{s}", [P, CH], I32) for s in range(SLOTS)]
        dst_f = sb("m_dst_f", [P, BATCHES * CH], F32)
        iota = sb("m_iota", [P, P], BF16)
        rel = [sb(f"m_rel{i}", [P, CH], F32) for i in range(3)]
        hot = [sb(f"m_hot{i}", [P, CH, P], BF16) for i in range(3)]
        wqkv = sb("m_wqkv", [P, 2, 3 * D], F32)
        wproj = sb("m_wproj", [P, 2, D], F32)
        bqkv = sb("m_bqkv", [P, 3 * D], F32)
        bias = sb("m_bias", [P, 2, D], F32)
        temp = sb("m_temp", [P, H], F32)
        weight = sb("m_weight", [P, H, 5], F32)
        wtmp = sb("m_wtmp", [P, H, 5], F32)
        temp2 = sb("m_temp2", [P, H], F32)
        xr = [sb(f"m_x{u}", [P, D], F32) for u in range(2)]
        xt = [sb(f"m_xt{u}", [P, 2, P], F32) for u in range(2)]
        held = sb("m_held", [1, 2], F32)
        qk = sb("m_qk", [P, 2 * D], F32)
        square = sb("m_square", [P, 2 * D], F32)
        norm2 = sb("m_norm2", [P, 2 * H], F32)
        norm = sb("m_norm", [P, 2 * H], F32)
        normc = sb("m_normc", [P, 2 * H], F32)
        inv = sb("m_inv", [P, 2 * H], F32)
        v1 = [sb(f"m_v1{u}", [P, H, 1 + HD], F32) for u in range(2)]
        kext = sb("m_kext", [P, H, EXT], F32)
        qext = [sb(f"m_qext{u}", [P, H, EXT], F32) for u in range(2)]
        quad = [sb(f"m_quad{g}", [P, 4, QUAD], F32) for g in range(2)]
        dst_i = quad[0][:, :, :].rearrange("p a b -> p (a b)").bitcast(I32)[:, 0:BATCHES * CH]
        tail = sb("m_tail", [P, H, TAIL], F32)
        msum = sb("m_msum", [P, 4, QUAD + TAIL], F32)
        mnum = sb("m_mnum", [P, H, 5, HD], F32)
        mden = sb("m_mden", [P, H, 5, HD], F32)
        qt = [sb(f"m_qt{g}", [P, 4, 4, P], F32) for g in range(2)]
        qtail = [sb(f"m_qtail{g}", [TAIL, 4, P], F32) for g in range(2)]
        rden = [sb(f"m_rden{g}", [P, P], F32) for g in range(2)]
        ot = [sb(f"m_ot{g}", [P, P], F32) for g in range(2)]
        mixo = [sb(f"m_mixo{u}", [P, D], F32) for u in range(2)]

        bank = [ctx.enter_context(nc.psum_tensor(f"m_bank{i}", [P, 512], F32)) for i in range(8)]
        ps_tail, ps_xq, ps_kv, ps_g = bank[4], bank[5], bank[6], bank[7]
        nd = [bank[5], bank[6]]
        ps_out = bank[5][:, D:2 * D]

        idx_in = [sem(f"m_idx_in{s}") for s in range(SLOTS)]
        gathered = [sem(f"m_gathered{s}") for s in range(SLOTS)]
        w_in = sem("m_w_in")
        hold_done = sem("m_hold_done")
        consts = sem("m_consts")
        rel_ready, hot_ready, first_done = sem("m_rel_ready"), sem("m_hot_ready"), sem("m_first_done")
        g_taken, batch_done = sem("m_g_taken"), sem("m_batch_done")
        more_rel = sem("m_more_rel")
        more_ready, more_done, more_taken = sem("m_more_ready"), sem("m_more_done"), sem("m_more_taken")
        x_in, q_out, xt_out = two("m_x_in"), two("m_q_out"), two("m_xt_out")
        xt_ps, xt_ready, qkv_ps = sem("m_xt_ps"), sem("m_xt_ready"), sem("m_qkv_ps")
        qk_ready, sq_ready, n2_ready, n_ready = sem("m_qk_ready"), sem("m_sq_ready"), sem("m_n2_ready"), sem("m_n_ready")
        ext_ready, ext2_ready, qext_ready = sem("m_ext_ready"), sem("m_ext2_ready"), sem("m_qext_ready")
        feat_ready, lin_ready, keys_done = sem("m_feat_ready"), sem("m_lin_ready"), sem("m_keys_done")
        msum_ready, mt_ps, m_ready = sem("m_msum_ready"), sem("m_mt_ps"), sem("m_m_ready")
        qx_in, xc_in = two("m_qx_in"), two("m_xc_in")
        qfeat_ready, qlin_ready = sem("m_qfeat_ready"), sem("m_qlin_ready")
        t_ps, t_copied, nd_ps, o_ready, proj_ps, mix_ready = (
            sem("m_t_ps"), sem("m_t_copied"), sem("m_nd_ps"), sem("m_o_ready"), sem("m_proj_ps"), sem("m_mix_ready"))
        mix_out = two("m_mix_out")
        dve = sem("m_dve")
        wdve = sem("m_wdve")

        def batches_of(turn, u, t, phase):
            if phase == 0:
                return t, (2 * u, turn), (2 * u + 1, turn)
            first = PAIRS + turn + u
            return t + TILES, ((2 + 2 * u) % SLOTS, first), ((3 + 2 * u) % SLOTS, first)

        def later(t):
            return not isinstance(t, int) or t > 0

        def before(turn, u):
            return (turn, 0) if u else (turn - 1, 1)

        def turned(ps, n, rows):
            return ps[:, 0:n * P].rearrange("p (k r) -> p k r", k=n)[0:rows, :, :]

        with nc.Block() as block:

            @block.sync
            def _(e):
                def load(n):
                    for s in range(SLOTS):
                        wait(e, gathered[s], n * (16 * CH))
                        e.dma_start(idx[s][:, :], A["src_cols"][:, bass.ds((n * SLOTS + s) * CH, CH)]).then_inc(idx_in[s], 16)

                load(0)
                e.dma_start(dst_i, A["dst_cols"]).then_inc(w_in, 16)
                for k in range(2):
                    e.dma_start(wqkv[:, k, :], A["wqkv"][k * P:(k + 1) * P, :]).then_inc(w_in, 16)
                    e.dma_start(wproj[:, k, :], A["wproj"][k * P:(k + 1) * P, :]).then_inc(w_in, 16)
                e.dma_start(bqkv[:, :], A["bqkv"].partition_broadcast(P)).then_inc(w_in, 16)
                e.dma_start(bias[:, 0, :], A["bproj"].partition_broadcast(P)).then_inc(w_in, 16)
                e.dma_start(bias[:, 1, :], A["gbias"].partition_broadcast(P)).then_inc(w_in, 16)
                e.dma_start(temp[:, :], A["temp"].partition_broadcast(P)).then_inc(w_in, 16)
                with e.Fori(1, BATCHES // SLOTS) as n:
                    load(n)

            @block.gpsimd
            def _(e):
                last_row = e.alloc_register("last_row")
                e.reg_mov(last_row, N)
                e.memset(held[:, :], 0.0).then_inc(hold_done, 1)

                def gather(n):
                    for s in range(SLOTS):
                        e.wait_ge(idx_in[s], n * 16 + 16)
                        wait(e, batch_done, n * SLOTS + (s + 1 - SLOTS))
                        hold(e, held, hold_done, n * SLOTS + s)
                        for j in range(CH):
                            e.indirect_dma_start(out=ring[s][:, j, :], out_offset=None, in_=d_table[:, :],
                                                 in_offset=bass.IndirectOffsetOnAxis(ap=idx[s][:, j:j + 1], axis=0),
                                                 bounds_check=last_row, oob_is_err=False).then_inc(gathered[s], 16)

                gather(0)
                with e.Fori(1, BATCHES // SLOTS) as n:
                    gather(n)

            @block.tensor
            def _(e):
                further = e.alloc_register("pe_further")
                e.reg_mov(further, 1)
                eye = cst[:, C_EYE:C_EYE + P]

                def edges(s, n, extra):
                    b = n * SLOTS + s

                    def product(h):
                        for j in range(CH):
                            for part in range(3):
                                width = SUMS if part == 2 else D
                                last = nc.tensor.matmul(ps_g[:, 0:width], h[:, j, :],
                                                        ring[s][:, j, part * D:part * D + width],
                                                        start=(j == 0 and part == 0), stop=(j == CH - 1 and part == 2),
                                                        skip_group_check=True)
                        return last

                    taken = e.snap(further, min_val=1, max_val=1 << 14)
                    e.wait_ge(gathered[s], n * (16 * CH) + 16 * CH)
                    e.wait_ge(hot_ready, b + 1)
                    wait(e, g_taken, b)
                    e.wait_ge(more_taken, taken)
                    product(hot[s % 2]).then_inc(first_done, 1)
                    with e.If(extra > 0):
                        with e.Fori(0, extra):
                            count = e.snap(further, min_val=1, max_val=1 << 14)
                            e.wait_ge(g_taken, b + 1)
                            e.wait_ge(more_ready, count)
                            e.wait_ge(more_taken, count)
                            product(hot[2]).then_inc(more_done, 1)
                            e.reg_add(further, further, 1)

                def turn_rows(u, t, count):
                    e.wait_ge(x_in[u], count)
                    wait(e, xt_ready, t)
                    wait(e, qk_ready, t)
                    for k in range(2):
                        last = nc.tensor.transpose(ps_xq[:, k * P:(k + 1) * P], xr[u][:, k * P:(k + 1) * P], eye)
                    last.then_inc(xt_ps, 1)

                def key_sums(u, t, rows):
                    e.wait_ge(feat_ready, t + 1)
                    e.wait_ge(lin_ready, t + 1)
                    for h in range(H):
                        o = 64 * (h % 2)
                        nc.tensor.matmul(bank[h // 2][o:o + 1 + HD, :], v1[u][0:rows, h, :], quad[h // 4][0:rows, h % 4, :],
                                         start=False, stop=False, skip_group_check=True, tile_position=(0, o))
                    for h in range(H):
                        o = 64 * (h % 2)
                        last = nc.tensor.matmul(ps_tail[o:o + 1 + HD, (h // 2) * P:(h // 2) * P + TAIL], v1[u][0:rows, h, :],
                                                tail[0:rows, h, :], start=False, stop=False, skip_group_check=True,
                                                tile_position=(0, o))
                    last.then_inc(keys_done, 1)

                def keys(turn, u, t, rows):
                    pair, (s1, n1), (s2, n2) = batches_of(turn, u, t, 0)
                    (_, more1), (_, more2) = windows_of(nc, e, win, pair)
                    e.wait_ge(xt_ready, t + 1)
                    for k in range(2):
                        nc.tensor.matmul(ps_xq[:, D:2 * D], xt[u][:, k, :], wqkv[:, k, 0:D],
                                         start=(k == 0), stop=(k == 1))
                    for k in range(2):
                        last = nc.tensor.matmul(ps_kv[:, :], xt[u][:, k, :], wqkv[:, k, D:3 * D],
                                                start=(k == 0), stop=(k == 1))
                    last.then_inc(qkv_ps, 1)
                    edges(s1, n1, more1)
                    if later(t):
                        key_sums(1 - u, t - 1, P)
                    if rows == P:
                        turn_rows(1 - u, t + 1, (turn + u) * 16 + 16)
                    edges(s2, n2, more2)

                def turn_features(g, t):
                    e.wait_ge(qfeat_ready, t * 2 + (1 + g))
                    for i in range(4):
                        wait(e, t_copied, t * 10 + (5 * g - 4 + i if i < 3 else 5 * g))
                        if i == 3:
                            e.wait_ge(qfeat_ready, t * 2 + 2)
                            e.wait_ge(qlin_ready, t + 1)
                        for c in range(4):
                            last = nc.tensor.transpose(bank[i][:, c * P:(c + 1) * P], quad[g][:, i, c * P:(c + 1) * P], eye)
                        last.then_inc(t_ps, 1)
                    for i in range(4):
                        last = nc.tensor.transpose(ps_tail[0:TAIL, i * P:(i + 1) * P], tail[:, 4 * g + i, :], eye)
                    last.then_inc(t_ps, 1)

                def sums_and_normalizers(g, t):
                    e.wait_ge(t_copied, t * 10 + (5 * g + 5))
                    wait(e, o_ready if g else mix_ready, t * 2 if g else t)
                    for o, m in ((0, mnum), (P, mden)):
                        for c in range(5):
                            for i in range(4):
                                k = P if c < 4 else TAIL
                                f = qt[g][:, i, c, :] if c < 4 else qtail[g][:, i, :]
                                last = nc.tensor.matmul(nd[g][32 * i:32 * i + 32, o:o + P], m[0:k, 4 * g + i, c, :], f,
                                                        start=(c == 0), stop=(c == 4), skip_group_check=True,
                                                        tile_position=(0, 32 * i))
                    last.then_inc(nd_ps, 1)

                def project(t):
                    e.wait_ge(o_ready, t * 2 + 2)
                    for g in range(2):
                        last = nc.tensor.matmul(ps_out, ot[g][:, :], wproj[:, g, :], start=(g == 0), stop=(g == 1))
                    last.then_inc(proj_ps, 1)

                def outputs(turn, u, t, rows):
                    pair, (s1, n1), (s2, n2) = batches_of(turn, u, t, 1)
                    (_, more1), (_, more2) = windows_of(nc, e, win, pair)
                    turn_features(0, t)
                    if later(t):
                        project(t - 1)
                    edges(s1, n1, more1)
                    turn_features(1, t)
                    sums_and_normalizers(0, t)
                    edges(s2, n2, more2)
                    sums_and_normalizers(1, t)

                e.wait_ge(consts, 1)
                e.wait_ge(w_in, 16 * 9)
                turn_rows(0, 0, 16)
                tile_loop(e, keys)
                key_sums(0, TILES - 1, LAST)
                e.wait_ge(msum_ready, 1)
                for p in range(4):
                    for c in range(4):
                        nc.tensor.transpose(bank[p][:, c * P:c * P + 97], msum[0:97, p, c * P:(c + 1) * P],
                                            cst[0:97, C_EYE:C_EYE + 97])
                    last = nc.tensor.transpose(ps_tail[0:TAIL, p * P:p * P + 97], msum[0:97, p, QUAD:QUAD + TAIL],
                                               cst[0:97, C_EYE:C_EYE + 97])
                last.then_inc(mt_ps, 1)
                e.wait_ge(m_ready, 1)
                tile_loop(e, outputs)
                project(TILES - 1)

            @block.scalar
            def _(e):
                def load_x(t, u, sem):
                    e.dma_start(xr[u][:, :], rows_of(d_xn, t, P, D)).then_inc(sem, 16)

                def rows_turned(turn, u, t):
                    e.wait_ge(xt_ps, t + 1)
                    wait(e, xt_out[u], turn * 16)
                    e.activation(xt[u][:, :, :], turned(ps_xq, 2, P), ACT.Copy).then_inc(xt_ready, 1)
                    e.wait_ge(xt_ready, t + 1)
                    e.dma_start(rows_of(d_xt, t, P, D), xt[u][:, :, :].rearrange("p k r -> p (k r)")).then_inc(xt_out[u], 16)

                def keys(turn, u, t, rows):
                    if rows == P:
                        wait(e, xt_ps, t)
                        load_x(t + 1, 1 - u, x_in[1 - u])
                    e.wait_ge(qk_ready, t + 1)
                    e.activation(square[:, :], qk[:, :], ACT.Square).then_inc(sq_ready, 1)
                    e.wait_ge(n2_ready, t + 1)
                    e.activation(norm[:, :], norm2[:, :], ACT.Sqrt).then_inc(n_ready, 1)
                    e.wait_ge(ext_ready, t + 1)
                    e.activation(kext[:, :, HD:EXT], kext[:, :, 0:16], ACT.Copy)
                    e.activation(qext[u][:, :, HD:EXT], qext[u][:, :, 0:16], ACT.Copy).then_inc(ext2_ready, 1)
                    wait(e, keys_done, t)
                    e.activation(tail[:, :, 0:HD], kext[:, :, 0:HD], ACT.Copy).then_inc(lin_ready, 1)
                    e.wait_ge(ext2_ready, t + 1)
                    e.dma_start(rows_of(d_q, t, P, H * EXT), qext[u][:, :, :].rearrange("p h c -> p (h c)")).then_inc(q_out[u], 16)
                    if rows == P:
                        rows_turned(turn + u, 1 - u, t + 1)

                def load_q(t, u):
                    e.dma_start(qext[u][:, :, :].rearrange("p h c -> p (h c)"), rows_of(d_q, t, P, H * EXT)).then_inc(qx_in[u], 16)

                def linear(turn, u, t):
                    e.wait_ge(qx_in[u], turn * 16 + 16)
                    wait(e, t_ps, t * 10)
                    e.activation(tail[:, :, 0:HD], qext[u][:, :, 0:HD], ACT.Copy).then_inc(qlin_ready, 1)

                def store(u, t):
                    e.wait_ge(mix_ready, t + 1)
                    e.dma_start(rows_of(d_mix, t, P, D), mixo[u][:, :]).then_inc(mix_out[u], 16)

                def outputs(turn, u, t, rows):
                    if rows == P:
                        wait(e, qlin_ready, t)
                        wait(e, qfeat_ready, t * 2)
                        load_q(t + 1, 1 - u)
                    wait(e, mix_ready, t - 1)
                    e.dma_start(xr[u][:, :], rows_of(A["x"], t, P, D)).then_inc(xc_in[u], 16)
                    for g in range(2):
                        wait(e, nd_ps, t * 2 + (g - 1))
                        for i in range(4):
                            e.wait_ge(t_ps, t * 10 + (5 * g + i + 1))
                            e.activation(qt[g][:, i, :, :], turned(bank[i], 4, P), ACT.Copy).then_inc(t_copied, 1)
                        e.wait_ge(t_ps, t * 10 + (5 * g + 5))
                        e.activation(qtail[g][:, :, :], turned(ps_tail, 4, TAIL), ACT.Copy).then_inc(t_copied, 1)
                    if rows == P:
                        linear(turn + u, 1 - u, t + 1)
                    if later(t):
                        store(1 - u, t - 1)

                load_x(0, 0, x_in[0])
                e.wait_ge(consts, 1)
                rows_turned(0, 0, 0)
                tile_loop(e, keys)
                for u in range(2):
                    e.wait_ge(q_out[u], 16 * (PAIRS + 1 - u))
                    e.wait_ge(xt_out[u], 16 * (PAIRS + 1 - u))
                e.wait_ge(keys_done, TILES)
                load_q(0, 0)
                linear(0, 0, 0)
                tile_loop(e, outputs)
                store(0, TILES - 1)
                for u in range(2):
                    e.wait_ge(mix_out[u], 16 * (PAIRS + 1 - u))

            @block.vector
            def _(e):
                further = e.alloc_register("dve_further")

                for i in range(5):
                    e.memset(bank[i][:, :], 0.0)
                e.memset(tail[:, :, TAIL - 1:TAIL], 1.0)
                for u in range(2):
                    e.memset(v1[u][:, :, 0:1], 1.0)
                e.memset(qext[0][:, :, :], 0.0)
                e.memset(qext[1][:, :, :], 0.0)
                e.memset(xt[0][:, :, :], 0.0)
                e.memset(xt[1][:, :, :], 0.0)
                e.memset(mixo[0][:, :], 0.0)
                e.memset(mixo[1][:, :], 0.0)
                e.tensor_copy(iota[:, :], cst[:, C_IOTA:C_IOTA + P])
                e.wait_ge(w_in, 16 * 9)
                e.tensor_copy(dst_f[:, :], dst_i).then_inc(wdve, 1)
                e.wait_ge(w_in, 16 * 9)
                e.tensor_tensor(temp2[:, :], temp[:, :], temp[:, :], ALU.mult).then_inc(wdve, 1)
                e.tensor_tensor(bias[:, 0, :], bias[:, 0, :], bias[:, 1, :], ALU.add).then_inc(wdve, 1)
                e.wait_ge(wdve, 3)
                column = lambda c: cst[:, c:c + 5].unsqueeze(1).broadcast_to([P, H, 5])
                e.tensor_tensor(weight[:, :, :], column(C_QUAD), temp2[:, :].unsqueeze(2).broadcast_to([P, H, 5]), ALU.mult)
                e.tensor_tensor(wtmp[:, :, :], column(C_LIN), temp[:, :].unsqueeze(2).broadcast_to([P, H, 5]),
                                ALU.mult).then_inc(wdve, 1)
                e.wait_ge(wdve, 4)
                e.tensor_tensor(weight[:, :, :], weight[:, :, :], wtmp[:, :, :], ALU.add).then_inc(wdve, 1)
                e.wait_ge(wdve, 5)
                e.tensor_tensor(weight[:, :, :], weight[:, :, :], column(C_ONE), ALU.add).then_inc(wdve, 1)
                e.reg_mov(further, 1)
                e.nop().then_inc(more_taken, 1)
                e.drain().then_inc(consts, 1)

                def compare(i, b, lo, relsem, count, outsem):
                    e.tensor_scalar(rel[i][:, :], dst_f[:, bass.ds(b * CH, CH)], cst[:, bass.ds(lo + C_WIN, 1)], None,
                                    ALU.subtract).then_inc(relsem, 1)
                    e.wait_ge(relsem, count)
                    for j in range(CH):
                        last = e.tensor_scalar(hot[i][:, j, :], iota[:, :], rel[i][:, j:j + 1], None, ALU.is_equal)
                    last.then_inc(outsem, 1)

                def add_sums(w, outsem):
                    e.tensor_tensor(agg[:, bass.ds(w, 1), :].squeeze(1), ps_g[:, 0:SUMS],
                                    agg[:, bass.ds(w, 1), :].squeeze(1), ALU.add).then_inc(outsem, 1)

                def first(s, n, lo):
                    b = n * SLOTS + s
                    wait(e, first_done, b - 1)
                    compare(s % 2, b, lo, rel_ready, b + 1, hot_ready)

                def finish(s, n, lo, extra):
                    b = n * SLOTS + s
                    with e.If(extra > 0):
                        count = e.snap(further, min_val=1, max_val=1 << 14)
                        compare(2, b, window(nc, e, lo + 1), more_rel, count, more_ready)
                    e.wait_ge(first_done, b + 1)
                    add_sums(lo, g_taken)
                    with e.If(extra > 0):
                        with e.Fori(0, extra) as w:
                            count = e.snap(further, min_val=1, max_val=1 << 14)
                            here = window(nc, e, lo + w + 1)
                            with e.If(w > 0):
                                compare(2, b, here, more_rel, count, more_ready)
                            e.wait_ge(more_done, count)
                            add_sums(here, more_taken)
                            e.reg_add(further, further, 1)
                    e.nop().then_inc(batch_done, 1)

                def products(x, g):
                    whole = x[:, 4 * g:4 * g + 4, :]
                    shifted = AP(whole.tensor, whole.offset, [list(whole.ap[0]), [EXT, 4], [1, 16], [1, HD]])
                    plain = x[:, 4 * g:4 * g + 4, 0:HD].unsqueeze(2).broadcast_to([P, 4, 16, HD])
                    return e.tensor_tensor(quad[g][:, :, :].rearrange("p h (s i) -> p h s i", i=HD), plain, shifted, ALU.mult)

                def tail_products(x):
                    return e.tensor_tensor(tail[:, :, HD:HD + 16], x[:, :, 0:16], x[:, :, 16:32], ALU.mult)

                def more_key_products():
                    products(kext, 1)
                    tail_products(kext).then_inc(feat_ready, 1)

                def keys(turn, u, t, rows):
                    pair, (s1, n1), (s2, n2) = batches_of(turn, u, t, 0)
                    (lo1, more1), (lo2, more2) = windows_of(nc, e, win, pair)
                    first(s1, n1, lo1)
                    if later(t):
                        more_key_products()
                    e.wait_ge(qkv_ps, t + 1)
                    e.tensor_tensor(qk[:, 0:D], ps_xq[:, D:2 * D], bqkv[:, 0:D], ALU.add)
                    e.tensor_tensor(qk[:, D:2 * D], ps_kv[:, 0:D], bqkv[:, D:2 * D], ALU.add)
                    heads = lambda ap: ap.rearrange("p (h c) -> p h c", c=HD)
                    wait(e, keys_done, t - 1)
                    e.tensor_tensor(v1[u][:, :, 1:1 + HD], heads(ps_kv[:, D:2 * D]), heads(bqkv[:, 2 * D:3 * D]),
                                    ALU.add).then_inc(qk_ready, 1)
                    first(s2, n2, lo2)
                    e.wait_ge(sq_ready, t + 1)
                    e.tensor_reduce(norm2[:, :], heads(square[:, :]), X, ALU.add).then_inc(n2_ready, 1)
                    finish(s1, n1, lo1, more1)
                    e.wait_ge(n_ready, t + 1)
                    e.tensor_scalar(normc[:, 0:H], norm[:, 0:H], SCALE, NORM_EPS, ALU.mult, ALU.max)
                    e.tensor_scalar(normc[:, H:2 * H], norm[:, H:2 * H], NORM_EPS, None, ALU.max).then_inc(dve, 1)
                    e.wait_ge(dve, t * 2 + 1)
                    e.reciprocal(inv[:, :], normc[:, :]).then_inc(dve, 1)
                    e.wait_ge(dve, t * 2 + 2)
                    wide = lambda a: inv[:, a:a + H].unsqueeze(2).broadcast_to([P, H, HD])
                    wait(e, lin_ready, t)
                    e.tensor_tensor(kext[:, :, 0:HD], heads(qk[:, D:2 * D]), wide(H), ALU.mult)
                    wait(e, q_out[u], turn * 16)
                    e.scalar_tensor_tensor(out=qext[u][:, :, 0:HD], in0=heads(qk[:, 0:D]), scalar=SCALE,
                                           in1=wide(0), op0=ALU.mult, op1=ALU.mult).then_inc(ext_ready, 1)
                    e.wait_ge(ext2_ready, t + 1)
                    wait(e, keys_done, t)
                    products(kext, 0)
                    finish(s2, n2, lo2, more2)

                def divide(g, t):
                    e.wait_ge(nd_ps, t * 2 + (g + 1))
                    e.reciprocal(rden[g][:, :], nd[g][:, P:2 * P]).then_inc(dve, 1)
                    e.wait_ge(dve, t * 3 + (2 * TILES + g + 1))
                    wait(e, proj_ps, t)
                    e.tensor_tensor(ot[g][:, :], nd[g][:, 0:P], rden[g][:, :], ALU.mult).then_inc(o_ready, 1)

                def add_input(turn, u, t):
                    e.wait_ge(proj_ps, t + 1)
                    wait(e, mix_out[u], turn * 16)
                    e.tensor_tensor(mixo[u][:, :], ps_out, bias[:, 0, :], ALU.add).then_inc(dve, 1)
                    e.wait_ge(dve, t * 3 + (2 * TILES + 3))
                    e.wait_ge(xc_in[u], turn * 16 + 16)
                    e.tensor_tensor(mixo[u][:, :], mixo[u][:, :], xr[u][:, :], ALU.add).then_inc(mix_ready, 1)

                def query_products(turn, u, t, g):
                    if g == 0:
                        e.wait_ge(qx_in[u], turn * 16 + 16)
                        wait(e, t_ps, t * 10 - 5)
                        products(qext[u], 0).then_inc(qfeat_ready, 1)
                    else:
                        wait(e, t_ps, t * 10)
                        products(qext[u], 1)
                        tail_products(qext[u]).then_inc(qfeat_ready, 1)

                def outputs(turn, u, t, rows):
                    pair, (s1, n1), (s2, n2) = batches_of(turn, u, t, 1)
                    (lo1, more1), (lo2, more2) = windows_of(nc, e, win, pair)
                    first(s1, n1, lo1)
                    if later(t):
                        divide(1, t - 1)
                    if rows == P:
                        query_products(turn + u, 1 - u, t + 1, 0)
                    if later(t):
                        before_turn, before_u = before(turn, u)
                        add_input(before_turn, before_u, t - 1)
                    finish(s1, n1, lo1, more1)
                    first(s2, n2, lo2)
                    if rows == P:
                        query_products(turn + u, 1 - u, t + 1, 1)
                    divide(0, t)
                    finish(s2, n2, lo2, more2)

                tile_loop(e, keys)
                more_key_products()
                e.wait_ge(keys_done, TILES)
                for p in range(4):
                    e.tensor_copy(msum[0:97, p, 0:QUAD], bank[p][0:97, :])
                e.tensor_copy(msum[0:97, :, QUAD:QUAD + TAIL],
                              ps_tail[0:97, :].rearrange("p (a b) -> p a b", a=4)[:, :, 0:TAIL]).then_inc(msum_ready, 1)
                query_products(0, 0, 0, 0)
                e.wait_ge(mt_ps, 1)
                for h in range(H):
                    src = bank[h // 2][:, :].rearrange("p (c b) -> p c b", b=P)[:, :, 64 * (h % 2):64 * (h % 2) + 1 + HD]
                    w = weight[:, h, 0:4].unsqueeze(2).broadcast_to([P, 4, HD])
                    e.tensor_tensor(mnum[:, h, 0:4, :], src[:, :, 1:1 + HD], w, ALU.mult)
                    e.tensor_tensor(mden[:, h, 0:4, :], src[:, :, 0:1].broadcast_to([P, 4, HD]), w, ALU.mult)
                for half in range(2):
                    src = ps_tail[0:TAIL, :].rearrange("p (a b) -> p a b", b=P)[:, :, 64 * half:64 * half + 1 + HD]
                    of_half = lambda m: m[0:TAIL, :, 4, :].rearrange("p (a b) c -> p a b c", b=2)[:, :, half, :]
                    w = weight[0:TAIL, :, 4].rearrange("p (a b) -> p a b", b=2)[:, :, half:half + 1].broadcast_to([TAIL, 4, HD])
                    e.tensor_tensor(of_half(mnum), src[:, :, 1:1 + HD], w, ALU.mult)
                    last = e.tensor_tensor(of_half(mden), src[:, :, 0:1].broadcast_to([TAIL, 4, HD]), w, ALU.mult)
                last.then_inc(m_ready, 1)
                query_products(0, 0, 0, 1)
                tile_loop(e, outputs)
                divide(1, TILES - 1)
                add_input(PAIRS, 0, TILES - 1)


def node_stage(nc, A, cst, agg, pos, units, ends, d_xt, d_mix, d_x1, d_slot):
    B = 4
    with ExitStack() as ctx:
        sb = lambda name, shape, dt: ctx.enter_context(nc.sbuf_tensor(name, shape, dt))
        sem = lambda name: ctx.enter_context(nc.semaphore(name))
        each = lambda name: [sem(f"{name}{u}") for u in range(B)]
        wgnn = sb("g_w", [P, 4, D], F32)
        wg = sb("g_wg", [P, 2, NX], F32)
        bg = sb("g_bg", [P, NX], F32)
        upper = sb("g_upper", [P, P], BF16)
        ones = sb("g_ones", [P, P], BF16)
        zero = sb("g_zero", [P, 2, D], F32)
        eps = sb("g_eps", [P, 1], F32)
        held = sb("g_held", [1, 4], F32)
        pheld = sb("g_pheld", [1, 2], F32)
        taken = sb("g_taken", [P, NX], F32)
        xt = [sb(f"g_xt{u}", [P, 2, P], F32) for u in range(B)]
        mix = [sb(f"g_mix{u}", [P, D], F32) for u in range(B)]
        deg = sb("g_deg", [P, TILES], F32)
        rdeg = sb("g_rdeg", [P, TILES], F32)
        mean = sb("g_mean", [P, D], F32)
        meant = sb("g_meant", [P, 2, P], F32)
        dump = sb("g_dump", [P, D], F32)
        ss = sb("g_ss", [P, 1], F32)
        norm = sb("g_norm", [P, 1], F32)
        rnorm = sb("g_rnorm", [P, 1], F32)
        x1 = [sb(f"g_x1{u}", [P, D], F32) for u in range(B)]
        stats = sb("g_stats", [P, 6], F32)
        mv = sb("g_mv", [P, 2], F32)
        std = sb("g_std", [P, 1], F32)
        rstd = sb("g_rstd", [P, 1], F32)
        x2 = [sb(f"g_x2{u}", [P, D], F32) for u in range(B)]
        x2t = sb("g_x2t", [P, 2, P], F32)
        score = sb("g_score", [P, NX], F32)
        best = sb("g_best", [P, NX], F32)
        which = sb("g_which", [P, NX], U32)
        whichf = sb("g_whichf", [P, 2], F32)
        chosen = sb("g_chosen", [P, 2, NX], F32)
        mask = sb("g_mask", [P, NX], BF16)
        rank = sb("g_rank", [P, NX], F32)
        slots = sb("g_slots", [P, 2, NX], F32)
        slotf = sb("g_slotf", [P, 2], F32)
        sidx = [sb(f"g_sidx{u}", [P, 2], I32) for u in range(B)]
        cnt = sb("g_cnt", [P, NX], F32)
        cnti = sb("g_cnti", [P, NX], I32)
        unit8 = sb("g_unit8", [P, NX], I32)
        up = sb("g_up", [P, NX], F32)
        posf = sb("g_posf", [P, 2 * TILES], F32)
        rowf = sb("g_rowf", [P, 2 * TILES], F32)
        moved = sb("g_moved", [P, 2 * TILES], F32)
        bank = [ctx.enter_context(nc.psum_tensor(f"g_bank{i}", [P, 512], F32)) for i in range(6)]
        ps_a, ps_b, ps_s, ps_r = bank[0:4]
        ps_o = bank[4:6]

        w_in, consts = sem("g_w_in"), sem("g_consts")
        hold_done = sem("g_hold_done")
        rows_in, x1_out = each("g_rows_in"), each("g_x1_out")
        slot_out = each("g_slot_out")
        rdeg_ready, rnorm_ready, rstd_ready = sem("g_rdeg_ready"), sem("g_rnorm_ready"), sem("g_rstd_ready")
        stats_ready, score_ready, which_ready = sem("g_stats_ready"), sem("g_score_ready"), sem("g_which_ready")
        number_ready = sem("g_number_ready")
        mean_ready, a_ps, at_ready, o_ps = sem("g_mean_ready"), sem("g_a_ps"), sem("g_at_ready"), sem("g_o_ps")
        ss_ready, norm_ready, x1_ready = sem("g_ss_ready"), sem("g_norm_ready"), sem("g_x1_ready")
        var_ready, std_ready, x2_ready = sem("g_var_ready"), sem("g_std_ready"), sem("g_x2_ready")
        b_ps, bt_ready, s_ps, mask_ready, r_ps = sem("g_b_ps"), sem("g_bt_ready"), sem("g_s_ps"), sem("g_mask_ready"), sem("g_r_ps")
        slot_ready, tile_done, ends_ready, zero_out = sem("g_slot_ready"), sem("g_tile_done"), sem("g_ends_ready"), sem("g_zero_out")
        best_ready, chosen_ready, rank_ready = sem("g_best_ready"), sem("g_chosen_ready"), sem("g_rank_ready")
        slots_ready, slotf_ready, pos_ready, fin = sem("g_slots_ready"), sem("g_slotf_ready"), sem("g_pos_ready"), sem("g_fin")

        def later(t):
            return not isinstance(t, int) or t > 0

        def turned(ps):
            return ps[:, 0:2 * P].rearrange("p (k r) -> p k r", k=2)

        with nc.Block() as block:

            @block.sync
            def _(e):
                for k in range(4):
                    e.dma_start(wgnn[:, k, :], A["wgnn"][k * P:(k + 1) * P, :]).then_inc(w_in, 16)
                for k in range(2):
                    e.dma_start(wg[:, k, :], A["wg"][k * P:(k + 1) * P, :]).then_inc(w_in, 16)
                e.dma_start(bg[:, :], A["bg"].partition_broadcast(P)).then_inc(w_in, 16)

                def load(turn, u, t, rows):
                    wait(e, o_ps, t + (1 - B))
                    e.dma_start(xt[u][:, :, :].rearrange("p k r -> p (k r)"), rows_of(d_xt, t, P, D)).then_inc(rows_in[u], 16)
                    wait(e, x1_ready, t + (1 - B))
                    e.dma_start(mix[u][:, :], rows_of(d_mix, t, P, D)).then_inc(rows_in[u], 16)

                four_tile_loop(e, load)
                e.wait_ge(ends_ready, 1)
                for x in range(NX):
                    end = e.value_load(ends[0:1, x:x + 1], min_val=x * CAP, max_val=x * CAP + N)
                    e.dma_start(d_slot[bass.ds(end, 2 * P), :].rearrange("(j p) c -> p j c", p=P), zero[:, :, :]).then_inc(zero_out, 16)
                e.wait_ge(zero_out, 16 * NX)

            @block.gpsimd
            def _(e):
                last_slot = e.alloc_register("last_slot")
                e.reg_mov(last_slot, NX * CAP - 1)
                e.memset(pheld[:, :], 0.0).then_inc(hold_done, 1)

                def scatter(turn, u, t, rows):
                    e.wait_ge(slot_ready, t + 1)
                    hold(e, pheld, hold_done, t)
                    for k in range(2):
                        e.indirect_dma_start(out=d_slot[:, :], out_offset=bass.IndirectOffsetOnAxis(ap=sidx[u][0:rows, k:k + 1], axis=0),
                                             in_=x2[u][0:rows, :], in_offset=None, bounds_check=last_slot,
                                             oob_is_err=False).then_inc(slot_out[u], 16)

                four_tile_loop(e, scatter)
                for u in range(B):
                    e.wait_ge(slot_out[u], 32 * len(range(u, TILES, B)))

            @block.tensor
            def _(e):
                e.wait_ge(w_in, 16 * 7)
                e.wait_ge(consts, 1)
                eye = cst[:, C_EYE:C_EYE + P]

                def product(u, t, count):
                    e.wait_ge(mean_ready, t + 1)
                    wait(e, at_ready, t)
                    for k in range(2):
                        last = nc.tensor.transpose(ps_a[:, k * P:(k + 1) * P], mean[:, k * P:(k + 1) * P], eye)
                    last.then_inc(a_ps, 1)
                    e.wait_ge(rows_in[u], count)
                    wait(e, x1_ready, t - 1)
                    for k in range(2):
                        nc.tensor.matmul(ps_o[u % 2][:, 0:D], xt[u][:, k, :], wgnn[:, k, :], start=(k == 0), stop=False)
                    e.wait_ge(at_ready, t + 1)
                    for k in range(2):
                        last = nc.tensor.matmul(ps_o[u % 2][:, 0:D], meant[:, k, :], wgnn[:, 2 + k, :],
                                                start=False, stop=(k == 1))
                    last.then_inc(o_ps, 1)

                def ranks(t, rows):
                    e.wait_ge(mask_ready, t + 1)
                    wait(e, tile_done, t)
                    nc.tensor.matmul(ps_r[0:rows, 0:NX], upper[0:rows, 0:rows], mask[0:rows, :], start=True, stop=True)
                    nc.tensor.matmul(ps_r[:, NX:2 * NX], ones[0:rows, :], mask[0:rows, :], start=True, stop=True,
                                     skip_group_check=True).then_inc(r_ps, 1)

                def tile(turn, u, t, rows):
                    if rows == P:
                        product((u + 1) % B, t + 1, (turn + (u + 1) // B) * 32 + 32)
                    if later(t):
                        ranks(t - 1, P)
                    e.wait_ge(x2_ready, t + 1)
                    wait(e, bt_ready, t)
                    for k in range(2):
                        last = nc.tensor.transpose(ps_b[:, k * P:k * P + rows], x2[u][0:rows, k * P:(k + 1) * P],
                                                   cst[0:rows, C_EYE:C_EYE + rows])
                    last.then_inc(b_ps, 1)
                    e.wait_ge(bt_ready, t + 1)
                    wait(e, score_ready, t)
                    for k in range(2):
                        last = nc.tensor.matmul(ps_s[0:rows, 0:NX], x2t[:, k, 0:rows], wg[:, k, :], start=(k == 0), stop=(k == 1))
                    last.then_inc(s_ps, 1)

                product(0, 0, 32)
                four_tile_loop(e, tile)
                ranks(TILES - 1, LAST)

            @block.scalar
            def _(e):
                e.wait_ge(consts, 1)

                def mean_turned(t):
                    e.wait_ge(a_ps, t + 1)
                    e.activation(meant[:, :, :], turned(ps_a), ACT.Copy).then_inc(at_ready, 1)

                def output_norm(u, t):
                    e.wait_ge(o_ps, t + 1)
                    e.activation(dump[:, :], ps_o[u % 2][:, 0:D], ACT.Square, accum_out=ss[:, 0:1]).then_inc(ss_ready, 1)
                    e.wait_ge(ss_ready, t + 1)
                    wait(e, rnorm_ready, t)
                    e.activation(norm[:, :], ss[:, :], ACT.Sqrt).then_inc(norm_ready, 1)

                def tile(turn, u, t, rows):
                    if rows == P:
                        mean_turned(t + 1)
                    e.wait_ge(var_ready, t + 1)
                    e.activation(std[0:rows, :], mv[0:rows, 1:2], ACT.Sqrt, bias=eps[0:rows, 0:1]).then_inc(std_ready, 1)
                    e.dma_start(rows_of(d_x1, t, P, D), x1[u][:, :]).then_inc(x1_out[u], 16)
                    if rows == P:
                        output_norm((u + 1) % B, t + 1)
                    e.wait_ge(b_ps, t + 1)
                    e.activation(x2t[:, :, 0:rows], turned(ps_b)[:, :, 0:rows], ACT.Copy).then_inc(bt_ready, 1)

                mean_turned(0)
                output_norm(0, 0)
                four_tile_loop(e, tile)
                for u in range(B):
                    e.wait_ge(x1_out[u], 16 * len(range(u, TILES, B)))

            @block.vector
            def _(e):
                e.tensor_copy(upper[:, :], cst[:, C_UP:C_UP + P])
                e.tensor_copy(taken[:, :], cst[:, C_BASE:C_BASE + NX])
                e.memset(ones[:, :], 1.0)
                e.memset(zero[:, :, :], 0.0)
                e.memset(eps[:, :], LN_EPS)
                e.memset(pos[:, :, :], 0)
                for u in range(B):
                    e.memset(x1[u][:, :], 0.0)
                e.tensor_scalar(deg[:, :], agg[:, :, D], 1.0, None, ALU.max)
                e.drain().then_inc(consts, 1)
                e.wait_ge(consts, 1)
                e.reciprocal(rdeg[:, :], deg[:, :]).then_inc(rdeg_ready, 1)
                e.wait_ge(rdeg_ready, 1)
                e.wait_ge(w_in, 16 * 7)

                def own(i, sem, value):
                    e.wait_ge(sem, value)
                    e.memset(held[:, i:i + 1], 0.0)

                def means(t):
                    wait(e, a_ps, t)
                    e.tensor_scalar(mean[:, :], agg[:, bass.ds(t, 1), 0:D].squeeze(1), rdeg[:, bass.ds(t, 1)], None,
                                    ALU.mult).then_inc(mean_ready, 1)

                def scores(t, rows):
                    e.wait_ge(s_ps, t + 1)
                    e.tensor_tensor(score[0:rows, :], ps_s[0:rows, 0:NX], bg[0:rows, :], ALU.add).then_inc(score_ready, 1)

                def best_scores(t, rows):
                    own(0, score_ready, t + 1)
                    e.max(best[0:rows, :], score[0:rows, :]).then_inc(best_ready, 1)

                def best_experts(t, rows):
                    own(1, best_ready, t + 1)
                    e.max_index(which[0:rows, :], best[0:rows, :], score[0:rows, :]).then_inc(which_ready, 1)

                def expert_numbers(t, rows):
                    e.wait_ge(which_ready, t + 1)
                    e.tensor_copy(whichf[0:rows, :], which[0:rows, 0:2]).then_inc(number_ready, 1)

                def masks(t, rows):
                    e.wait_ge(number_ready, t + 1)
                    for k in range(2):
                        last = e.tensor_scalar(chosen[0:rows, k, :], cst[0:rows, C_E:C_E + NX], whichf[0:rows, k:k + 1],
                                               None, ALU.is_equal)
                    last.then_inc(chosen_ready, 1)
                    e.wait_ge(chosen_ready, t + 1)
                    e.tensor_tensor(mask[0:rows, :], chosen[0:rows, 0, :], chosen[0:rows, 1, :], ALU.add).then_inc(mask_ready, 1)

                def ranks(t, rows):
                    e.wait_ge(r_ps, t + 1)
                    e.tensor_tensor(rank[0:rows, :], ps_r[0:rows, 0:NX], taken[0:rows, :], ALU.add).then_inc(rank_ready, 1)
                    e.wait_ge(rank_ready, t + 1)
                    e.tensor_tensor(taken[:, :], ps_r[:, NX:2 * NX], taken[:, :], ALU.add).then_inc(tile_done, 1)
                    e.tensor_tensor(slots[0:rows, :, :], chosen[0:rows, :, :], rank[0:rows, :].unsqueeze(1).broadcast_to([rows, 2, NX]),
                                    ALU.mult).then_inc(slots_ready, 1)

                def slot_numbers(u, t, rows):
                    e.wait_ge(slots_ready, t + 1)
                    e.tensor_reduce(slotf[0:rows, :], slots[0:rows, :, :], X, ALU.add).then_inc(slotf_ready, 1)
                    e.wait_ge(slotf_ready, t + 1)
                    e.tensor_copy(sidx[u][0:rows, :], slotf[0:rows, :]).then_inc(slot_ready, 1)
                    e.tensor_copy(pos[0:rows, bass.ds(t, 1), :].squeeze(1), slotf[0:rows, :]).then_inc(pos_ready, 1)
                    e.wait_ge(tile_done, t + 1)

                def tile(turn, u, t, rows):
                    gate = later(t)
                    if rows == P:
                        means(t + 1)
                    e.wait_ge(norm_ready, t + 1)
                    e.reciprocal(rnorm[0:rows, :], norm[0:rows, :]).then_inc(rnorm_ready, 1)
                    if gate:
                        scores(t - 1, P)
                    e.wait_ge(rnorm_ready, t + 1)
                    e.wait_ge(rows_in[u], turn * 32 + 32)
                    wait(e, x1_out[u], turn * 16)
                    e.scalar_tensor_tensor(out=x1[u][0:rows, :], in0=ps_o[u % 2][0:rows, 0:D], scalar=rnorm[0:rows, 0:1],
                                           in1=mix[u][0:rows, :], op0=ALU.mult, op1=ALU.add).then_inc(x1_ready, 1)
                    if gate:
                        best_scores(t - 1, P)
                    own(2, x1_ready, t + 1)
                    e.bn_stats(stats[0:rows, :], x1[u][0:rows, :]).then_inc(stats_ready, 1)
                    if gate:
                        best_experts(t - 1, P)
                    own(3, stats_ready, t + 1)
                    e.bn_aggr(mv[0:rows, :], stats[0:rows, :]).then_inc(var_ready, 1)
                    if gate:
                        expert_numbers(t - 1, P)
                        masks(t - 1, P)
                    e.wait_ge(std_ready, t + 1)
                    e.reciprocal(rstd[0:rows, :], std[0:rows, :]).then_inc(rstd_ready, 1)
                    e.wait_ge(rstd_ready, t + 1)
                    wait(e, slot_out[u], turn * 32)
                    e.tensor_scalar(x2[u][0:rows, :], x1[u][0:rows, :], mv[0:rows, 0:1], rstd[0:rows, 0:1],
                                    ALU.subtract, ALU.mult).then_inc(x2_ready, 1)
                    if gate:
                        ranks(t - 1, P)
                        slot_numbers((u - 1) % B, t - 1, P)

                means(0)
                four_tile_loop(e, tile)
                t = TILES - 1
                scores(t, LAST)
                best_scores(t, LAST)
                best_experts(t, LAST)
                expert_numbers(t, LAST)
                masks(t, LAST)
                ranks(t, LAST)
                slot_numbers(t % B, t, LAST)
                e.wait_ge(pos_ready, TILES)
                e.tensor_tensor(cnt[:, :], taken[:, :], cst[:, C_BASE:C_BASE + NX], ALU.subtract)
                e.tensor_copy(ends[:, :], taken[0:1, :])
                e.tensor_copy(posf[:, :], pos[:, 0:TILES, :].rearrange("p t k -> p (t k)")).then_inc(fin, 1)
                e.wait_ge(fin, 1)
                e.tensor_scalar(cnti[:, :], cnt[:, :], UNIT - 1.0, float(UNIT), ALU.add, ALU.max).then_inc(fin, 1)
                e.wait_ge(fin, 2)
                e.tensor_scalar(unit8[:, :], cnti[:, :], 8, None, ALU.arith_shift_right).then_inc(fin, 1)
                e.wait_ge(fin, 3)
                e.tensor_copy(units[:, :], unit8[0:1, :])
                e.tensor_scalar(up[:, :], unit8[:, :], -float(UNIT), float(CAP), ALU.mult, ALU.add)
                e.tensor_copy(rowf[:, :], posf[:, :]).then_inc(fin, 1)
                e.wait_ge(fin, 4)
                for x in range(1, NX):
                    e.tensor_scalar(moved[:, :], posf[:, :], float(x * CAP), up[:, x - 1:x], ALU.is_ge, ALU.mult).then_inc(fin, 1)
                    e.wait_ge(fin, 3 + 2 * x)
                    e.tensor_tensor(rowf[:, :], rowf[:, :], moved[:, :], ALU.subtract).then_inc(fin, 1)
                    e.wait_ge(fin, 4 + 2 * x)
                e.tensor_copy(pos[:, 0:TILES, :].rearrange("p t k -> p (t k)"), rowf[:, :])
                e.drain().then_inc(ends_ready, 1)


def expert_stage(nc, A, cst, units, d_slot, d_y):
    U = UNIT
    KF = FF // P
    with ExitStack() as ctx:
        sb = lambda name, shape, dt: ctx.enter_context(nc.sbuf_tensor(name, shape, dt))
        sem = lambda name: ctx.enter_context(nc.semaphore(name))
        two = lambda name: [sem(f"{name}{u}") for u in range(2)]
        w1 = [sb(f"e_w1{u}", [P, 2, FF], F32) for u in range(2)]
        w2 = [sb(f"e_w2{u}", [P, KF, D], F32) for u in range(2)]
        b1 = [sb(f"e_b1{u}", [P, KF], F32) for u in range(2)]
        b2 = [sb(f"e_b2{u}", [P, D], F32) for u in range(2)]
        x = sb("e_x", [P, 2, D], F32)
        zero = sb("e_zero", [P, 2, D], F32)
        xt = sb("e_xt", [P, 2, U], F32)
        ht = sb("e_ht", [P, KF, U], F32)
        y = sb("e_y", [P, 2, D], F32)
        ps_x = ctx.enter_context(nc.psum_tensor("e_psx", [P, 2, U], F32))
        ps_h = [ctx.enter_context(nc.psum_tensor(f"e_psh{i}", [P, 512], F32)) for i in range(KF)]
        ps_y = [ctx.enter_context(nc.psum_tensor(f"e_psy{i}", [P, 512], F32)) for i in range(2)]
        w_in = two("e_w_in")
        x_in, y_out = sem("e_x_in"), sem("e_y_out")
        x_ps, xt_ready, h_ps, h_ready, y_ps, y_ready, y_free = (
            sem("e_x_ps"), sem("e_xt_ready"), sem("e_h_ps"), sem("e_h_ready"), sem("e_y_ps"), sem("e_y_ready"), sem("e_y_free"))
        expert_done, zero_ready = sem("e_expert_done"), sem("e_zero_ready")

        def experts(e, body):
            with e.Fori(0, NX // 2) as pair:
                for u in range(2):
                    body(pair, u, pair * 2 + u)

        def unit_loop(e, x, body):
            count = e.value_load(units[0:1, bass.ds(x, 1)], min_val=1, max_val=-(-N // U))
            with e.Fori(0, count) as i:
                body(i)

        class Turn:

            def __init__(self, e, name):
                self.e, self.reg = e, e.alloc_register(name)
                e.reg_mov(self.reg, 1)

            def now(self):
                return self.e.snap(self.reg, min_val=1, max_val=UNITS)

            def next(self):
                self.e.reg_add(self.reg, self.reg, 1)

        with nc.Block() as block:

            @block.sync
            def _(e):
                turn = Turn(e, "sp_unit")

                def weights(pair, u, x_):
                    e.wait_ge(expert_done, x_ + 1)
                    e.dma_start(w1[u][:, :, :], A["w1"][bass.ds(x_, 1), :, :].rearrange("o (k p) f -> p (o k) f", p=P)).then_inc(w_in[u], 16)
                    e.dma_start(w2[u][:, :, :], A["w2"][bass.ds(x_, 1), :, :].rearrange("o (k p) f -> p (o k) f", p=P)).then_inc(w_in[u], 16)
                    e.dma_start(b1[u][:, :], A["b1"][bass.ds(x_, 1), :, :].rearrange("o p k -> (o p) k")).then_inc(w_in[u], 16)
                    e.dma_start(b2[u][:, :], A["b2"][bass.ds(x_, 1), :].squeeze(0).partition_broadcast(P)).then_inc(w_in[u], 16)

                def expert(pair, u, x_):
                    weights(pair, u, x_)

                    def unit(i):
                        n = turn.now()
                        e.wait_ge(x_ps, n)
                        e.dma_start(x[:, :, :], d_slot[bass.ds(x_ * CAP + i * U, U), :].rearrange("(j p) c -> p j c", p=P)).then_inc(x_in, 16)
                        turn.next()

                    unit_loop(e, x_, unit)

                experts(e, expert)
                e.wait_ge(x_ps, turn.now())
                e.dma_start(x[:, :, :], d_slot[0:U, :].rearrange("(j p) c -> p j c", p=P)).then_inc(x_in, 16)

            @block.gpsimd
            def _(e):
                turn = Turn(e, "pool_unit")
                e.memset(zero[:, :, :], 0.0).then_inc(zero_ready, 1)
                e.wait_ge(zero_ready, 1)
                e.nop().then_inc(y_free, 1)

                def expert(pair, u, x_):
                    def unit(i):
                        n = turn.now()
                        e.wait_ge(y_ready, n + 1)
                        e.dma_start(d_y[bass.ds((n - 1) * U, U), :].rearrange("(j p) c -> p j c", p=P), y[:, :, :]).then_inc(y_out, 16)
                        e.wait_ge(y_out, n * 16)
                        e.nop().then_inc(y_free, 1)
                        turn.next()

                    unit_loop(e, x_, unit)

                experts(e, expert)
                with e.Fori(turn.now() - 1, UNITS) as n:
                    e.dma_start(d_y[bass.ds(n * U, U), :].rearrange("(j p) c -> p j c", p=P), zero[:, :, :]).then_inc(y_out, 16)
                    e.wait_ge(y_out, n * 16 + 16)

            @block.tensor
            def _(e):
                turn = Turn(e, "pe_unit")
                e.nop().then_inc(x_ps, 1)
                e.nop().then_inc(expert_done, 2)

                def rows_turned(n):
                    e.wait_ge(x_in, n * 16)
                    e.wait_ge(xt_ready, n)
                    for k in range(2):
                        for j in range(2):
                            last = nc.tensor.transpose(ps_x[:, k, j * P:(j + 1) * P], x[:, j, k * P:(k + 1) * P],
                                                       cst[:, C_EYE:C_EYE + P])
                    last.then_inc(x_ps, 1)

                def expert(pair, v, x_):
                    e.wait_ge(w_in[v], pair * 64 + 64)

                    def unit(i):
                        n = turn.now()
                        e.wait_ge(xt_ready, n + 1)
                        e.wait_ge(h_ready, n * KF - (KF - 1))
                        for c in range(KF):
                            for k in range(2):
                                last = nc.tensor.matmul(ps_h[c][:, 0:U], w1[v][:, k, c * P:(c + 1) * P], xt[:, k, :],
                                                        start=(k == 0), stop=(k == 1))
                            last.then_inc(h_ps, 1)
                        rows_turned(n + 1)
                        e.wait_ge(y_ready, n)
                        for c in range(KF):
                            e.wait_ge(h_ready, n * KF + (c + 2 - KF))
                            for j in range(2):
                                last = nc.tensor.matmul(ps_y[j][:, 0:D], ht[:, c, j * P:(j + 1) * P], w2[v][:, c, :],
                                                        start=(c == 0), stop=(c == KF - 1), skip_group_check=True)
                        last.then_inc(y_ps, 1)
                        turn.next()

                    unit_loop(e, x_, unit)

                rows_turned(turn.now())
                experts(e, expert)

            @block.scalar
            def _(e):
                turn = Turn(e, "act_unit")
                e.nop().then_inc(h_ready, 1)

                def expert(pair, v, x_):
                    e.wait_ge(w_in[v], pair * 64 + 64)

                    def unit(i):
                        n = turn.now()
                        e.wait_ge(y_ps, n)
                        for c in range(KF):
                            e.wait_ge(h_ps, n * KF + (c + 1 - KF))
                            e.activation(ht[:, c, :], ps_h[c][:, 0:U], ACT.Gelu, bias=b1[v][:, c:c + 1]).then_inc(h_ready, 1)
                        turn.next()

                    unit_loop(e, x_, unit)

                experts(e, expert)

            @block.vector
            def _(e):
                turn = Turn(e, "dve_unit")
                e.nop().then_inc(xt_ready, 1)
                e.nop().then_inc(y_ready, 1)
                e.nop().then_inc(y_ps, 1)

                def copy_rows(n):
                    e.wait_ge(x_ps, n + 1)
                    e.tensor_copy(xt[:, :, :], ps_x[:, :, :]).then_inc(xt_ready, 1)

                def expert(pair, v, x_):
                    e.wait_ge(w_in[v], pair * 64 + 64)

                    def unit(i):
                        n = turn.now()
                        copy_rows(n + 1)
                        e.wait_ge(y_free, n)
                        e.wait_ge(y_ps, n + 1)
                        for j in range(2):
                            last = e.tensor_tensor(y[:, j, :], ps_y[j][:, 0:D], b2[v][:, :], ALU.add)
                        last.then_inc(y_ready, 1)
                        turn.next()

                    unit_loop(e, x_, unit)
                    e.wait_ge(y_ready, turn.now())
                    e.nop().then_inc(expert_done, 1)

                copy_rows(turn.now())
                experts(e, expert)


def combine_stage(nc, A, pos, d_x1, d_y):
    B = 4
    with ExitStack() as ctx:
        sb = lambda name, shape, dt: ctx.enter_context(nc.sbuf_tensor(name, shape, dt))
        sem = lambda name: ctx.enter_context(nc.semaphore(name))
        each = lambda name: [sem(f"{name}{u}") for u in range(B)]
        idx = [sb(f"c_idx{u}", [P, 2], I32) for u in range(B)]
        x1 = [sb(f"c_x1{u}", [P, D], F32) for u in range(B)]
        ya = [sb(f"c_ya{u}", [P, D], F32) for u in range(B)]
        yb = [sb(f"c_yb{u}", [P, D], F32) for u in range(B)]
        part = [sb(f"c_part{u}", [P, D], F32) for u in range(B)]
        out = [sb(f"c_out{u}", [P, D], F32) for u in range(2)]
        held = sb("c_held", [1, 2], F32)
        hold_done = sem("c_hold_done")
        x_in, y_in = each("c_x_in"), each("c_y_in")
        out_done = [sem(f"c_out_done{u}") for u in range(2)]
        idx_ready, part_ready, added = sem("c_idx_ready"), sem("c_part_ready"), sem("c_added")

        with nc.Block() as block:

            @block.sync
            def _(e):
                def load(turn, u, t, rows):
                    wait(e, part_ready, t + (1 - B))
                    e.dma_start(x1[u][:, :], rows_of(d_x1, t, P, D)).then_inc(x_in[u], 16)

                four_tile_loop(e, load)

            @block.gpsimd
            def _(e):
                last_slot = e.alloc_register("last_slot2")
                e.reg_mov(last_slot, UNITS * UNIT - 1)
                e.memset(held[:, :], 0.0).then_inc(hold_done, 1)

                def gather(turn, u, t, rows):
                    e.wait_ge(idx_ready, t + 1)
                    wait(e, added, t + (1 - B))
                    hold(e, held, hold_done, t)
                    for k, y in ((0, ya), (1, yb)):
                        e.indirect_dma_start(out=y[u][0:rows, :], out_offset=None, in_=d_y[:, :],
                                             in_offset=bass.IndirectOffsetOnAxis(ap=idx[u][0:rows, k:k + 1], axis=0),
                                             bounds_check=last_slot, oob_is_err=False).then_inc(y_in[u], 16)

                four_tile_loop(e, gather)

            @block.scalar
            def _(e):
                def store(turn, u, t, rows):
                    e.wait_ge(added, t + 1)
                    e.dma_start(rows_of(A["out"], t, rows, D), out[u % 2][0:rows, :]).then_inc(out_done[u % 2], 16)

                four_tile_loop(e, store)
                for u in range(2):
                    e.wait_ge(out_done[u], 16 * len(range(u, TILES, 2)))

            @block.vector
            def _(e):
                def index(turn, u, t):
                    wait(e, y_in[u], turn * 32)
                    e.tensor_copy(idx[u][:, :], pos[:, bass.ds(t, 1), :].squeeze(1)).then_inc(idx_ready, 1)

                def add(turn, u, t, rows):
                    e.wait_ge(x_in[u], turn * 16 + 16)
                    e.wait_ge(y_in[u], turn * 32 + 32)
                    e.tensor_tensor(part[u][0:rows, :], x1[u][0:rows, :], ya[u][0:rows, :], ALU.add).then_inc(part_ready, 1)
                    e.wait_ge(part_ready, t + 1)
                    wait(e, out_done[u % 2], turn * 32 + 16 * (u // 2))
                    e.tensor_tensor(out[u % 2][0:rows, :], part[u][0:rows, :], yb[u][0:rows, :], ALU.add).then_inc(added, 1)
                    if not isinstance(t, int) or t + B < TILES:
                        index(turn + 1, u, t + B)

                for u in range(B):
                    index(0, u, u)
                four_tile_loop(e, add)


def kernel(x, src, dst, L0_gnn_weight, L0_gnn_bias, L0_mix_Wqkv, L0_mix_bqkv, L0_mix_Wproj, L0_mix_bproj,
           L0_mix_temperature, L0_ffn_Wg, L0_ffn_bg, L0_ffn_W1, L0_ffn_b1, L0_ffn_W2, L0_ffn_b2):
    import concourse.bacc as bacc
    from concourse.bass_utils import run_bass_kernel_spmd

    x = np.asarray(x)
    src, dst = np.asarray(src), np.asarray(dst)
    pad = BATCHES * CH * P - E
    src = np.concatenate([src, np.full(pad, N, src.dtype)])
    dst = np.concatenate([dst, dst[-pad:]])
    cols = lambda a: np.ascontiguousarray(a.reshape(BATCHES, CH, P).transpose(2, 0, 1).reshape(P, BATCHES * CH))
    arrays = {
        "x": np.concatenate([x, np.zeros((TILES * P - N, D), x.dtype)]),
        "src_cols": cols(src), "dst_cols": cols(dst), "dst_rows": dst.reshape(BATCHES // 2, 2 * CH * P),
        "cst": constants(),
        "wgnn": L0_gnn_weight, "gbias": L0_gnn_bias,
        "wqkv": np.asarray(L0_mix_Wqkv).T, "bqkv": L0_mix_bqkv,
        "wproj": np.asarray(L0_mix_Wproj).T, "bproj": L0_mix_bproj,
        "temp": np.asarray(L0_mix_temperature).reshape(H),
        "wg": L0_ffn_Wg, "bg": L0_ffn_bg,
        "w1": L0_ffn_W1, "b1": np.asarray(L0_ffn_b1).reshape(NX, FF // P, P).transpose(0, 2, 1), "w2": L0_ffn_W2, "b2": L0_ffn_b2,
    }
    arrays = {f"in_{k}": np.ascontiguousarray(a) for k, a in arrays.items()}
    nc = bacc.Bacc("TRN2", target_bir_lowering=False, num_devices=1)
    A = {k[3:]: nc.dram_tensor(k, a.shape, mybir.dt.from_np(a.dtype), kind="ExternalInput").ap() for k, a in arrays.items()}
    A["out"] = nc.dram_tensor("out", (N, D), F32, kind="ExternalOutput").ap()
    build(nc, A)
    r = run_bass_kernel_spmd(nc, [arrays], core_ids=[0])
    return r.results[0]["out"]
```

```python
from contextlib import ExitStack

import numpy as np

import concourse.bass as bass
from concourse import mybir
from concourse.bass import AP

F32 = mybir.dt.float32
BF16 = mybir.dt.bfloat16
I32 = mybir.dt.int32
U32 = mybir.dt.uint32
ALU = mybir.AluOpType
ACT = mybir.ActivationFunctionType
X = mybir.AxisListType.X

P = 128
N, D, E = 6250, 256, 200000
H, HD = 8, 32
TILES = -(-N // P)
LAST = N - (TILES - 1) * P
PAIRS = (TILES - 1) // 2
CH = 8
BATCHES = -(-E // (CH * P))
SLOTS = 4
ROW = 3 * D + 2
SUMS = D + 1
EXT = HD + 16
QUAD = 16 * HD
TAIL = HD + 16 + 1
NX, FF = 8, 512
CAP = 51 * P
UNIT = 2 * P
UNITS = (2 * N + NX * UNIT) // UNIT + 1
CODE = 64
SCALE = float(HD) ** 0.25
LN_EPS = 1e-5
NORM_EPS = 1e-12

C_EYE, C_UP, C_IOTA, C_WIN = 0, P, 2 * P, 3 * P
C_QUAD = C_WIN + TILES
C_LIN, C_ONE = C_QUAD + 5, C_QUAD + 10
C_E, C_BASE = C_QUAD + 15, C_QUAD + 15 + NX
C_ALL = C_BASE + NX


def constants():
    c = np.zeros((P, C_ALL), np.float32)
    c[:, C_EYE:C_EYE + P] = np.eye(P)
    c[:, C_UP:C_UP + P] = np.triu(np.ones((P, P)), 1)
    c[:, C_IOTA:C_IOTA + P] = np.arange(P)
    c[:, C_WIN:C_WIN + TILES] = P * np.arange(TILES)
    f = SCALE ** 4 / N
    c[:, C_QUAD:C_QUAD + 4] = f
    c[0:HD, C_QUAD] = 0.5 * f
    c[HD:HD + 16, C_QUAD + 4] = f
    c[0:HD, C_LIN + 4] = f
    c[HD + 16, C_ONE + 4] = f
    c[:, C_E:C_E + NX] = np.arange(NX)
    c[:, C_BASE:C_BASE + NX] = CAP * np.arange(NX)
    return c


def wait(e, sem, value):
    if not isinstance(value, int) or value > 0:
        e.wait_ge(sem, value)


def hold(pool, held):
    pool.nop().then_inc(held, 1)


def rows_of(dram, tile, rows, width):
    return dram[bass.ds(tile * P, rows), 0:width]


def window(nc, e, value):
    return nc.s_assert_within(e.snap(value), 0, TILES - 1,
                              skip_runtime_bounds_check_because="edges end at nodes, and nodes are in windows below TILES")


def windows_of(nc, e, win, pair):
    code = e.value_load(win[0:1, bass.ds(pair, 1)], min_val=0, max_val=CODE ** 4 - 1)
    digit = lambda i: window(nc, e, (code >> (6 * i)) & (CODE - 1))
    return (digit(0), digit(1)), (digit(2), digit(3))


def tile_loop(e, body):
    for u in range(2):
        body(0, u, u, P)
    with e.Fori(1, PAIRS) as turn:
        for u in range(2):
            body(turn, u, turn * 2 + u, P)
    body(PAIRS, 0, TILES - 1, LAST)


def four_tile_loop(e, body):
    for u in range(4):
        body(0, u, u, P)
    with e.Fori(1, TILES // 4) as turn:
        for u in range(4):
            body(turn, u, turn * 4 + u, P)
    body(TILES // 4, 0, TILES - 1, LAST)


def build(nc, A):
    dram = lambda name, shape, dt: nc.dram_tensor(name, shape, dt, kind="Internal").ap()
    d_xn = dram("d_xn", [TILES * P, D], F32)
    d_table = dram("d_table", [N + 1, ROW], BF16)
    d_win = dram("d_win", [BATCHES // 2, 1], I32)
    d_q = dram("d_q", [TILES * P, H * EXT], F32)
    d_xt = dram("d_xt", [TILES * P, D], F32)
    d_ot = dram("d_ot", [TILES * P, D], F32)
    d_x1 = dram("d_x1", [TILES * P, D], F32)
    d_slot = dram("d_slot", [NX * CAP, D], F32)
    d_y = dram("d_y", [UNITS * UNIT, D], F32)

    with ExitStack() as whole:
        ws = lambda name, shape, dt: whole.enter_context(nc.sbuf_tensor(name, shape, dt))
        cst = ws("cst", [P, C_ALL], F32)
        win = ws("win", [1, BATCHES // 2], I32)
        agg = ws("agg", [P, TILES, SUMS], F32)
        pos = ws("pos", [P, TILES + 3, 2], I32)
        units = ws("units", [1, NX], I32)
        ends = ws("ends", [1, NX], I32)
        hold_done = whole.enter_context(nc.semaphore("hold_done"))
        node_weights = (ws("g_w", [P, 4, D], F32), ws("g_wproj", [P, 2, D], F32), ws("g_bias", [P, 2, D], F32),
                        ws("g_wg", [P, 2, NX], F32), ws("g_bg", [P, NX], F32))
        norm_stage(nc, A, cst, win, agg, d_xn, d_table, d_win)
        mix_stage(nc, A, cst, win, agg, d_xn, d_table, d_q, d_xt, d_ot, node_weights, hold_done)
        expert_weights = tuple([ws(f"{name}{u}", shape, F32) for u in range(2)] for name, shape in (
            ("e_w1", [P, 2, FF]), ("e_w2", [P, FF // P, D]), ("e_b1", [P, FF // P]), ("e_b2", [P, D])))
        w_in = [whole.enter_context(nc.semaphore(f"e_w_in{u}")) for u in range(2)]
        node_stage(nc, A, cst, agg, pos, units, ends, d_xt, d_ot, d_x1, d_slot, node_weights, hold_done,
                   expert_weights, w_in)
        expert_stage(nc, A, cst, units, d_slot, d_y, expert_weights, w_in)
        combine_stage(nc, A, pos, d_x1, d_y, hold_done)


def norm_stage(nc, A, cst, win, agg, d_xn, d_table, d_win):
    G = 4
    GROUPS = (TILES - 1) // G
    HALF = BATCHES // 2
    with ExitStack() as ctx:
        sb = lambda name, shape, dt: ctx.enter_context(nc.sbuf_tensor(name, shape, dt))
        sem = lambda name: ctx.enter_context(nc.semaphore(name))
        xg = [sb(f"n_x{u}", [P, G, D], F32) for u in range(2)]
        xn = [sb(f"n_xn{u}", [P, G, D], F32) for u in range(2)]
        rest = [sb(f"n_rest{u}", [P, G, D], F32) for u in range(2)]
        tab = [sb(f"n_tab{u}", [P, G, ROW], BF16) for u in range(2)]
        stats = sb("n_stats", [P, G, 6], F32)
        mv = sb("n_mv", [P, G, 2], F32)
        std = sb("n_std", [P, G], F32)
        rstd = sb("n_rstd", [P, G], F32)
        eps = sb("n_eps", [P, 1], F32)
        held = sb("n_held", [1, 1], F32)
        zero = sb("n_zero", [1, ROW], BF16)
        dst = sb("n_dst", [HALF, 2, CH * P], I32)
        ext = sb("n_ext", [HALF, 2, 2], I32)
        shifted = sb("n_shift", [HALF, 2, 2], I32)
        extra = sb("n_extra", [HALF, 2], I32)
        extra64 = sb("n_extra64", [HALF, 2], I32)
        code = sb("n_code", [HALF, 2], I32)
        code2 = sb("n_code2", [HALF, 1], I32)
        codes = sb("n_codes", [HALF, 1], I32)

        x_in = [sem(f"n_x_in{u}") for u in range(2)]
        table_out = [sem(f"n_table_out{u}") for u in range(2)]
        xn_out = [sem(f"n_xn_out{u}") for u in range(2)]
        cst_in, dst_in, zero_out = sem("n_cst_in"), sem("n_dst_in"), sem("n_zero_out")
        win_moved = sem("n_win_moved")
        ready = sem("n_ready")
        dve = sem("n_dve")
        var_ready, std_ready = sem("n_var_ready"), sem("n_std_ready")
        xn_ready, high_ready = sem("n_xn_ready"), sem("n_high_ready")
        rest_ready, mid_ready = sem("n_rest_ready"), sem("n_mid_ready")
        low_ready, agg_cleared = sem("n_low_ready"), sem("n_agg_cleared")
        codes_ready, stats_ready, rstd_ready = sem("n_codes_ready"), sem("n_stats_ready"), sem("n_rstd_ready")

        def groups(e, body):
            for u in range(2):
                body(0, u, u, G, P)
            with e.Fori(1, GROUPS // 2) as turn:
                for u in range(2):
                    body(turn, u, turn * 2 + u, G, P)
            body(GROUPS // 2, 0, GROUPS, 1, LAST)

        def node_rows(dram, g, n, rows):
            if n == 1:
                return dram[bass.ds(g * G * P, rows), :]
            return dram[bass.ds(g * G * P, G * P), :].rearrange("(j p) c -> p j c", p=P)

        def tiles_of(buf, n, rows):
            return buf[0:rows, 0, :] if n == 1 else buf[:, :, :]

        with nc.Block() as block:

            @block.sync
            def _(e):
                e.dma_start(cst[:, :], A["cst"]).then_inc(cst_in, 16)
                e.dma_start(dst[:, :, :], A["dst_rows"].rearrange("p (j c) -> p j c", j=2)).then_inc(dst_in, 16)

                def load(turn, u, g, n, rows):
                    wait(e, xn_ready, g - 1)
                    e.dma_start(tiles_of(xg[u], n, P), node_rows(A["x"], g, n, P)).then_inc(x_in[u], 16)

                groups(e, load)
                e.wait_ge(codes_ready, 1)
                e.dma_start(d_win[:, :], codes[:, :]).then_inc(win_moved, 16)
                e.wait_ge(win_moved, 16)
                e.dma_start(win[0:1, :], d_win.rearrange("(o p) c -> o (p c)", o=1)).then_inc(win_moved, 16)
                e.wait_ge(win_moved, 32)
                e.wait_ge(cst_in, 16)

            @block.gpsimd
            def _(e):
                def store(turn, u, g, n, rows):
                    e.wait_ge(xn_ready, g + 1)
                    e.dma_start(node_rows(d_xn, g, n, P), tiles_of(xn[u], n, P)).then_inc(xn_out[u], 16)
                    e.wait_ge(mid_ready, g + 1)
                    e.tensor_tensor(tab[u][:, 0:n, 2 * D:3 * D], rest[u][:, 0:n, :],
                                    tab[u][:, 0:n, D:2 * D], ALU.subtract).then_inc(low_ready, 1)
                    e.wait_ge(low_ready, g + 1)
                    e.dma_start(node_rows(d_table, g, n, rows), tiles_of(tab[u], n, rows)).then_inc(table_out[u], 16)

                e.memset(agg[:, :, :], 0.0).then_inc(agg_cleared, 1)
                e.wait_ge(agg_cleared, 1)
                e.wait_ge(ready, 1)
                e.dma_start(d_table[N:N + 1, :], zero[0:1, :]).then_inc(zero_out, 16)
                groups(e, store)
                for u, uses in ((0, GROUPS // 2 + 1), (1, GROUPS // 2)):
                    e.wait_ge(xn_out[u], 16 * uses)
                    e.wait_ge(table_out[u], 16 * uses)
                e.wait_ge(zero_out, 16)

            @block.scalar
            def _(e):
                e.wait_ge(ready, 1)

                def deviations(g):
                    e.wait_ge(var_ready, g + 1)
                    e.activation(std[:, :], mv[:, :, 1], ACT.Sqrt, bias=eps[:, 0:1]).then_inc(std_ready, 1)

                def parts(turn, u, g, n, rows):
                    e.wait_ge(xn_ready, g + 1)
                    wait(e, table_out[u], turn * 16)
                    e.activation(tab[u][:, 0:n, 0:D], xn[u][:, 0:n, :], ACT.Copy).then_inc(high_ready, 1)
                    if n > 1:
                        deviations(g + 1)
                    e.wait_ge(rest_ready, g + 1)
                    e.activation(tab[u][:, 0:n, D:2 * D], rest[u][:, 0:n, :], ACT.Copy).then_inc(mid_ready, 1)

                deviations(0)
                groups(e, parts)

            @block.vector
            def _(e):
                e.memset(eps[:, :], LN_EPS)
                e.memset(zero[:, :], 0.0)
                for u in range(2):
                    e.memset(tab[u][:, :, 3 * D:3 * D + 1], 1.0)
                    e.memset(tab[u][:, :, 3 * D + 1:ROW], 0.0)
                e.drain().then_inc(ready, 1)

                e.wait_ge(dst_in, 16)
                e.tensor_reduce(ext[:, :, 0], dst[:, :, :], X, ALU.min)
                e.tensor_reduce(ext[:, :, 1], dst[:, :, :], X, ALU.max).then_inc(dve, 1)
                e.wait_ge(dve, 1)
                e.tensor_scalar(shifted[:, :, :], ext[:, :, :], 7, None, ALU.arith_shift_right).then_inc(dve, 1)
                e.wait_ge(dve, 2)
                e.tensor_tensor(extra[:, :], shifted[:, :, 1], shifted[:, :, 0], ALU.subtract).then_inc(dve, 1)
                e.wait_ge(dve, 3)
                e.tensor_scalar(extra64[:, :], extra[:, :], float(CODE), None, ALU.mult).then_inc(dve, 1)
                e.wait_ge(dve, 4)
                e.tensor_tensor(code[:, :], extra64[:, :], shifted[:, :, 0], ALU.add).then_inc(dve, 1)
                e.wait_ge(dve, 5)
                e.tensor_scalar(code2[:, :], code[:, 1:2], float(CODE * CODE), None, ALU.mult).then_inc(dve, 1)
                e.wait_ge(dve, 6)
                e.tensor_tensor(codes[:, :], code2[:, :], code[:, 0:1], ALU.add).then_inc(codes_ready, 1)

                def statistics(g, u, count, n):
                    e.wait_ge(x_in[u], count)
                    for j in range(n):
                        last = e.bn_stats(stats[:, j, :], xg[u][:, j, :])
                    last.then_inc(stats_ready, 1)
                    e.wait_ge(stats_ready, g + 1)
                    wait(e, xn_ready, g)
                    e.memset(held[:, :], 0.0)
                    for j in range(n):
                        last = e.bn_aggr(mv[:, j, :], stats[:, j, :])
                    last.then_inc(var_ready, 1)

                def rows_norm(turn, u, g, n, rows):
                    e.wait_ge(std_ready, g + 1)
                    e.reciprocal(rstd[:, 0:n], std[:, 0:n]).then_inc(rstd_ready, 1)
                    e.wait_ge(rstd_ready, g + 1)
                    wait(e, xn_out[u], turn * 16)
                    for j in range(n):
                        last = e.tensor_scalar(xn[u][:, j, :], xg[u][:, j, :], mv[:, j, 0:1],
                                               rstd[:, j:j + 1], ALU.subtract, ALU.mult)
                    last.then_inc(xn_ready, 1)
                    if n > 1:
                        statistics(g + 1, 1 - u, (turn + u) * 16 + 16, G)
                    e.wait_ge(high_ready, g + 1)
                    wait(e, low_ready, g - 1)
                    e.tensor_tensor(rest[u][:, 0:n, :], xn[u][:, 0:n, :], tab[u][:, 0:n, 0:D],
                                    ALU.subtract).then_inc(rest_ready, 1)

                statistics(0, 0, 16, G)
                groups(e, rows_norm)


def mix_stage(nc, A, cst, win, agg, d_xn, d_table, d_q, d_xt, d_ot, node_weights, hold_done):
    with ExitStack() as ctx:
        sb = lambda name, shape, dt: ctx.enter_context(nc.sbuf_tensor(name, shape, dt))
        sem = lambda name: ctx.enter_context(nc.semaphore(name))
        two = lambda name: [sem(f"{name}{u}") for u in range(2)]
        ring = [sb(f"m_ring{s}", [P, CH, ROW], BF16) for s in range(SLOTS)]
        idx = [sb(f"m_idx{s}", [P, CH], I32) for s in range(SLOTS)]
        dst_f = sb("m_dst_f", [P, BATCHES * CH], F32)
        iota = sb("m_iota", [P, P], BF16)
        rel = [sb(f"m_rel{i}", [P, CH], F32) for i in range(3)]
        hot = [sb(f"m_hot{i}", [P, CH, P], BF16) for i in range(3)]
        wqkv = sb("m_wqkv", [P, 2, 3 * D], F32)
        bqkv = sb("m_bqkv", [P, 3 * D], F32)
        temp = sb("m_temp", [P, H], F32)
        weight = sb("m_weight", [P, H, 5], F32)
        wtmp = sb("m_wtmp", [P, H, 5], F32)
        temp2 = sb("m_temp2", [P, H], F32)
        xr = [sb(f"m_x{u}", [P, D], F32) for u in range(2)]
        xt = [sb(f"m_xt{u}", [P, 2, P], F32) for u in range(2)]
        qk = sb("m_qk", [P, 2 * D], F32)
        square = sb("m_square", [P, 2 * D], F32)
        norm2 = sb("m_norm2", [P, 2 * H], F32)
        norm = sb("m_norm", [P, 2 * H], F32)
        normc = sb("m_normc", [P, 2 * H], F32)
        inv = sb("m_inv", [P, 2 * H], F32)
        v1 = [sb(f"m_v1{u}", [P, H, 1 + HD], F32) for u in range(2)]
        kext = sb("m_kext", [P, H, EXT], F32)
        qext = [sb(f"m_qext{u}", [P, H, EXT], F32) for u in range(2)]
        quad = [sb(f"m_quad{g}", [P, 4, QUAD], F32) for g in range(2)]
        dst_i = quad[0][:, :, :].rearrange("p a b -> p (a b)").bitcast(I32)[:, 0:BATCHES * CH]
        tail = sb("m_tail", [P, H, TAIL], F32)
        msum = sb("m_msum", [P, 4, QUAD + TAIL], F32)
        mnum = sb("m_mnum", [P, H, 5, HD], F32)
        mden = sb("m_mden", [P, H, 5, HD], F32)
        qt = [sb(f"m_qt{g}", [P, 4, 4, P], F32) for g in range(2)]
        qtail = [sb(f"m_qtail{g}", [TAIL, 4, P], F32) for g in range(2)]
        rden = [sb(f"m_rden{g}", [P, P], F32) for g in range(2)]
        ot = [sb(f"m_ot{u}", [P, 2, P], F32) for u in range(2)]

        bank = [ctx.enter_context(nc.psum_tensor(f"m_bank{i}", [P, 512], F32)) for i in range(8)]
        ps_tail, ps_xq, ps_kv, ps_g = bank[4], bank[5], bank[6], bank[7]
        nd = [bank[5], bank[6]]

        idx_in = [sem(f"m_idx_in{s}") for s in range(SLOTS)]
        gathered = [sem(f"m_gathered{s}") for s in range(SLOTS)]
        w_in, node_w_in = sem("m_w_in"), sem("m_node_w_in")
        wgnn, wproj, bias, wg, bg = node_weights
        consts = sem("m_consts")
        rel_ready, hot_ready, first_done = sem("m_rel_ready"), sem("m_hot_ready"), sem("m_first_done")
        g_taken, batch_done = sem("m_g_taken"), sem("m_batch_done")
        more_rel = sem("m_more_rel")
        more_ready, more_done, more_taken = sem("m_more_ready"), sem("m_more_done"), sem("m_more_taken")
        x_in, q_out, xt_out = two("m_x_in"), two("m_q_out"), two("m_xt_out")
        xt_ps, xt_ready, qkv_ps = sem("m_xt_ps"), sem("m_xt_ready"), sem("m_qkv_ps")
        qk_ready, sq_ready, n2_ready, n_ready = sem("m_qk_ready"), sem("m_sq_ready"), sem("m_n2_ready"), sem("m_n_ready")
        ext_ready, ext2_ready = sem("m_ext_ready"), sem("m_ext2_ready")
        feat_ready, lin_ready, keys_done = sem("m_feat_ready"), sem("m_lin_ready"), sem("m_keys_done")
        msum_ready, mt_ps, m_ready = sem("m_msum_ready"), sem("m_mt_ps"), sem("m_m_ready")
        qx_in = two("m_qx_in")
        qfeat_ready, qlin_ready = sem("m_qfeat_ready"), sem("m_qlin_ready")
        t_ps, t_copied, nd_ps, o_ready = sem("m_t_ps"), sem("m_t_copied"), sem("m_nd_ps"), sem("m_o_ready")
        ot_out = two("m_ot_out")
        dve = sem("m_dve")
        wdve = sem("m_wdve")

        def batches_of(turn, u, t, phase):
            if phase == 0:
                return t, (2 * u, turn), (2 * u + 1, turn)
            first = PAIRS + turn + u
            return t + TILES, ((2 + 2 * u) % SLOTS, first), ((3 + 2 * u) % SLOTS, first)

        def later(t):
            return not isinstance(t, int) or t > 0

        def before(turn, u):
            return (turn, 0) if u else (turn - 1, 1)

        def turned(ps, n, rows):
            return ps[:, 0:n * P].rearrange("p (k r) -> p k r", k=n)[0:rows, :, :]

        with nc.Block() as block:

            @block.sync
            def _(e):
                def load(n):
                    for s in range(SLOTS):
                        wait(e, gathered[s], n * (16 * CH))
                        e.dma_start(idx[s][:, :], A["src_cols"][:, bass.ds((n * SLOTS + s) * CH, CH)]).then_inc(idx_in[s], 16)

                load(0)
                e.dma_start(dst_i, A["dst_cols"]).then_inc(w_in, 16)
                for k in range(2):
                    e.dma_start(wqkv[:, k, :], A["wqkv"][k * P:(k + 1) * P, :]).then_inc(w_in, 16)
                e.dma_start(bqkv[:, :], A["bqkv"].partition_broadcast(P)).then_inc(w_in, 16)
                e.dma_start(temp[:, :], A["temp"].partition_broadcast(P)).then_inc(w_in, 16)
                for k in range(4):
                    e.dma_start(wgnn[:, k, :], A["wgnn"][k * P:(k + 1) * P, :]).then_inc(node_w_in, 16)
                e.dma_start(bias[:, 0, :], A["bproj"].partition_broadcast(P)).then_inc(node_w_in, 16)
                e.dma_start(bias[:, 1, :], A["gbias"].partition_broadcast(P)).then_inc(node_w_in, 16)
                for k in range(2):
                    e.dma_start(wproj[:, k, :], A["wproj"][k * P:(k + 1) * P, :]).then_inc(node_w_in, 16)
                    e.dma_start(wg[:, k, :], A["wg"][k * P:(k + 1) * P, :]).then_inc(node_w_in, 16)
                e.dma_start(bg[:, :], A["bg"].partition_broadcast(P)).then_inc(node_w_in, 16)
                with e.Fori(1, BATCHES // SLOTS) as n:
                    load(n)
                e.wait_ge(node_w_in, 16 * 11)

            @block.gpsimd
            def _(e):
                last_row = e.alloc_register("last_row")
                e.reg_mov(last_row, N)

                def gather(n):
                    for s in range(SLOTS):
                        e.wait_ge(idx_in[s], n * 16 + 16)
                        wait(e, batch_done, n * SLOTS + (s + 1 - SLOTS))
                        hold(e, hold_done)
                        for j in range(CH):
                            e.indirect_dma_start(out=ring[s][:, j, :], out_offset=None, in_=d_table[:, :],
                                                 in_offset=bass.IndirectOffsetOnAxis(ap=idx[s][:, j:j + 1], axis=0),
                                                 bounds_check=last_row, oob_is_err=False).then_inc(gathered[s], 16)

                gather(0)
                with e.Fori(1, BATCHES // SLOTS) as n:
                    gather(n)

            @block.tensor
            def _(e):
                further = e.alloc_register("pe_further")
                e.reg_mov(further, 1)
                eye = cst[:, C_EYE:C_EYE + P]

                def edges(s, n, extra):
                    b = n * SLOTS + s

                    def product(h):
                        for j in range(CH):
                            for part in range(3):
                                width = SUMS if part == 2 else D
                                last = nc.tensor.matmul(ps_g[:, 0:width], h[:, j, :],
                                                        ring[s][:, j, part * D:part * D + width],
                                                        start=(j == 0 and part == 0), stop=(j == CH - 1 and part == 2),
                                                        skip_group_check=True)
                        return last

                    taken = e.snap(further, min_val=1, max_val=1 << 14)
                    e.wait_ge(gathered[s], n * (16 * CH) + 16 * CH)
                    e.wait_ge(hot_ready, b + 1)
                    wait(e, g_taken, b)
                    e.wait_ge(more_taken, taken)
                    product(hot[s % 2]).then_inc(first_done, 1)
                    with e.If(extra > 0):
                        with e.Fori(0, extra):
                            count = e.snap(further, min_val=1, max_val=1 << 14)
                            e.wait_ge(g_taken, b + 1)
                            e.wait_ge(more_ready, count)
                            e.wait_ge(more_taken, count)
                            product(hot[2]).then_inc(more_done, 1)
                            e.reg_add(further, further, 1)

                def turn_rows(u, t, count):
                    e.wait_ge(x_in[u], count)
                    wait(e, xt_ready, t)
                    wait(e, qk_ready, t)
                    for k in range(2):
                        last = nc.tensor.transpose(ps_xq[:, k * P:(k + 1) * P], xr[u][:, k * P:(k + 1) * P], eye)
                    last.then_inc(xt_ps, 1)

                def key_sums(u, t, rows):
                    e.wait_ge(feat_ready, t + 1)
                    e.wait_ge(lin_ready, t + 1)
                    for h in range(H):
                        o = 64 * (h % 2)
                        nc.tensor.matmul(bank[h // 2][o:o + 1 + HD, :], v1[u][0:rows, h, :], quad[h // 4][0:rows, h % 4, :],
                                         start=False, stop=False, skip_group_check=True, tile_position=(0, o))
                    for h in range(H):
                        o = 64 * (h % 2)
                        last = nc.tensor.matmul(ps_tail[o:o + 1 + HD, (h // 2) * P:(h // 2) * P + TAIL], v1[u][0:rows, h, :],
                                                tail[0:rows, h, :], start=False, stop=False, skip_group_check=True,
                                                tile_position=(0, o))
                    last.then_inc(keys_done, 1)

                def keys(turn, u, t, rows):
                    pair, (s1, n1), (s2, n2) = batches_of(turn, u, t, 0)
                    (_, more1), (_, more2) = windows_of(nc, e, win, pair)
                    e.wait_ge(xt_ready, t + 1)
                    for k in range(2):
                        nc.tensor.matmul(ps_xq[:, D:2 * D], xt[u][:, k, :], wqkv[:, k, 0:D],
                                         start=(k == 0), stop=(k == 1))
                    for k in range(2):
                        last = nc.tensor.matmul(ps_kv[:, :], xt[u][:, k, :], wqkv[:, k, D:3 * D],
                                                start=(k == 0), stop=(k == 1))
                    last.then_inc(qkv_ps, 1)
                    edges(s1, n1, more1)
                    if later(t):
                        key_sums(1 - u, t - 1, P)
                    if rows == P:
                        turn_rows(1 - u, t + 1, (turn + u) * 16 + 16)
                    edges(s2, n2, more2)

                def turn_features(g, t):
                    e.wait_ge(qfeat_ready, t * 2 + (1 + g))
                    for i in range(4):
                        wait(e, t_copied, t * 10 + (5 * g - 4 + i if i < 3 else 5 * g))
                        if i == 3:
                            e.wait_ge(qfeat_ready, t * 2 + 2)
                            e.wait_ge(qlin_ready, t + 1)
                        for c in range(4):
                            last = nc.tensor.transpose(bank[i][:, c * P:(c + 1) * P], quad[g][:, i, c * P:(c + 1) * P], eye)
                        last.then_inc(t_ps, 1)
                    for i in range(4):
                        last = nc.tensor.transpose(ps_tail[0:TAIL, i * P:(i + 1) * P], tail[:, 4 * g + i, :], eye)
                    last.then_inc(t_ps, 1)

                def sums_and_normalizers(g, t):
                    e.wait_ge(t_copied, t * 10 + (5 * g + 5))
                    wait(e, o_ready, t * 2 + (g - 1))
                    for o, m in ((0, mnum), (P, mden)):
                        for c in range(5):
                            for i in range(4):
                                k = P if c < 4 else TAIL
                                f = qt[g][:, i, c, :] if c < 4 else qtail[g][:, i, :]
                                last = nc.tensor.matmul(nd[g][32 * i:32 * i + 32, o:o + P], m[0:k, 4 * g + i, c, :], f,
                                                        start=(c == 0), stop=(c == 4), skip_group_check=True,
                                                        tile_position=(0, 32 * i))
                    last.then_inc(nd_ps, 1)

                def outputs(turn, u, t, rows):
                    pair, (s1, n1), (s2, n2) = batches_of(turn, u, t, 1)
                    (_, more1), (_, more2) = windows_of(nc, e, win, pair)
                    turn_features(0, t)
                    edges(s1, n1, more1)
                    turn_features(1, t)
                    sums_and_normalizers(0, t)
                    edges(s2, n2, more2)
                    sums_and_normalizers(1, t)

                e.wait_ge(consts, 1)
                e.wait_ge(w_in, 16 * 5)
                turn_rows(0, 0, 16)
                tile_loop(e, keys)
                key_sums(0, TILES - 1, LAST)
                e.wait_ge(msum_ready, 1)
                for p in range(4):
                    for c in range(4):
                        nc.tensor.transpose(bank[p][:, c * P:c * P + 97], msum[0:97, p, c * P:(c + 1) * P],
                                            cst[0:97, C_EYE:C_EYE + 97])
                    last = nc.tensor.transpose(ps_tail[0:TAIL, p * P:p * P + 97], msum[0:97, p, QUAD:QUAD + TAIL],
                                               cst[0:97, C_EYE:C_EYE + 97])
                last.then_inc(mt_ps, 1)
                e.wait_ge(m_ready, 1)
                tile_loop(e, outputs)

            @block.scalar
            def _(e):
                def load_x(t, u, sem):
                    e.dma_start(xr[u][:, :], rows_of(d_xn, t, P, D)).then_inc(sem, 16)

                def rows_turned(turn, u, t):
                    e.wait_ge(xt_ps, t + 1)
                    wait(e, xt_out[u], turn * 16)
                    e.activation(xt[u][:, :, :], turned(ps_xq, 2, P), ACT.Copy).then_inc(xt_ready, 1)
                    e.wait_ge(xt_ready, t + 1)
                    e.dma_start(rows_of(d_xt, t, P, D), xt[u][:, :, :].rearrange("p k r -> p (k r)")).then_inc(xt_out[u], 16)

                def keys(turn, u, t, rows):
                    if rows == P:
                        wait(e, xt_ps, t)
                        load_x(t + 1, 1 - u, x_in[1 - u])
                    e.wait_ge(qk_ready, t + 1)
                    e.activation(square[:, :], qk[:, :], ACT.Square).then_inc(sq_ready, 1)
                    e.wait_ge(n2_ready, t + 1)
                    e.activation(norm[:, :], norm2[:, :], ACT.Sqrt).then_inc(n_ready, 1)
                    e.wait_ge(ext_ready, t + 1)
                    e.activation(kext[:, :, HD:EXT], kext[:, :, 0:16], ACT.Copy)
                    e.activation(qext[u][:, :, HD:EXT], qext[u][:, :, 0:16], ACT.Copy).then_inc(ext2_ready, 1)
                    wait(e, keys_done, t)
                    e.activation(tail[:, :, 0:HD], kext[:, :, 0:HD], ACT.Copy).then_inc(lin_ready, 1)
                    e.wait_ge(ext2_ready, t + 1)
                    e.dma_start(rows_of(d_q, t, P, H * EXT), qext[u][:, :, :].rearrange("p h c -> p (h c)")).then_inc(q_out[u], 16)
                    if rows == P:
                        rows_turned(turn + u, 1 - u, t + 1)

                def load_q(t, u):
                    e.dma_start(qext[u][:, :, :].rearrange("p h c -> p (h c)"), rows_of(d_q, t, P, H * EXT)).then_inc(qx_in[u], 16)

                def linear(turn, u, t):
                    e.wait_ge(qx_in[u], turn * 16 + 16)
                    wait(e, t_ps, t * 10)
                    e.activation(tail[:, :, 0:HD], qext[u][:, :, 0:HD], ACT.Copy).then_inc(qlin_ready, 1)

                def store(u, t):
                    e.wait_ge(o_ready, t * 2 + 2)
                    e.dma_start(rows_of(d_ot, t, P, D), ot[u][:, :, :].rearrange("p k r -> p (k r)")).then_inc(ot_out[u], 16)

                def outputs(turn, u, t, rows):
                    if rows == P:
                        wait(e, qlin_ready, t)
                        wait(e, qfeat_ready, t * 2)
                        load_q(t + 1, 1 - u)
                    for g in range(2):
                        wait(e, nd_ps, t * 2 + (g - 1))
                        for i in range(4):
                            e.wait_ge(t_ps, t * 10 + (5 * g + i + 1))
                            e.activation(qt[g][:, i, :, :], turned(bank[i], 4, P), ACT.Copy).then_inc(t_copied, 1)
                        e.wait_ge(t_ps, t * 10 + (5 * g + 5))
                        e.activation(qtail[g][:, :, :], turned(ps_tail, 4, TAIL), ACT.Copy).then_inc(t_copied, 1)
                    if rows == P:
                        linear(turn + u, 1 - u, t + 1)
                    if later(t):
                        store(1 - u, t - 1)

                load_x(0, 0, x_in[0])
                e.wait_ge(consts, 1)
                rows_turned(0, 0, 0)
                tile_loop(e, keys)
                for u in range(2):
                    e.wait_ge(q_out[u], 16 * (PAIRS + 1 - u))
                    e.wait_ge(xt_out[u], 16 * (PAIRS + 1 - u))
                e.wait_ge(keys_done, TILES)
                load_q(0, 0)
                linear(0, 0, 0)
                tile_loop(e, outputs)
                store(0, TILES - 1)
                for u in range(2):
                    e.wait_ge(ot_out[u], 16 * (PAIRS + 1 - u))

            @block.vector
            def _(e):
                further = e.alloc_register("dve_further")

                for i in range(5):
                    e.memset(bank[i][:, :], 0.0)
                e.memset(tail[:, :, TAIL - 1:TAIL], 1.0)
                for u in range(2):
                    e.memset(v1[u][:, :, 0:1], 1.0)
                e.memset(qext[0][:, :, :], 0.0)
                e.memset(qext[1][:, :, :], 0.0)
                e.memset(xt[0][:, :, :], 0.0)
                e.memset(xt[1][:, :, :], 0.0)
                e.tensor_copy(iota[:, :], cst[:, C_IOTA:C_IOTA + P])
                e.wait_ge(w_in, 16 * 5)
                e.tensor_copy(dst_f[:, :], dst_i).then_inc(wdve, 1)
                e.wait_ge(w_in, 16 * 5)
                e.tensor_tensor(temp2[:, :], temp[:, :], temp[:, :], ALU.mult).then_inc(wdve, 1)
                e.wait_ge(wdve, 2)
                column = lambda c: cst[:, c:c + 5].unsqueeze(1).broadcast_to([P, H, 5])
                e.tensor_tensor(weight[:, :, :], column(C_QUAD), temp2[:, :].unsqueeze(2).broadcast_to([P, H, 5]), ALU.mult)
                e.tensor_tensor(wtmp[:, :, :], column(C_LIN), temp[:, :].unsqueeze(2).broadcast_to([P, H, 5]),
                                ALU.mult).then_inc(wdve, 1)
                e.wait_ge(wdve, 3)
                e.tensor_tensor(weight[:, :, :], weight[:, :, :], wtmp[:, :, :], ALU.add).then_inc(wdve, 1)
                e.wait_ge(wdve, 4)
                e.tensor_tensor(weight[:, :, :], weight[:, :, :], column(C_ONE), ALU.add).then_inc(wdve, 1)
                e.reg_mov(further, 1)
                e.nop().then_inc(more_taken, 1)
                e.drain().then_inc(consts, 1)

                def compare(i, b, lo, relsem, count, outsem):
                    e.tensor_scalar(rel[i][:, :], dst_f[:, bass.ds(b * CH, CH)], cst[:, bass.ds(lo + C_WIN, 1)], None,
                                    ALU.subtract).then_inc(relsem, 1)
                    e.wait_ge(relsem, count)
                    for j in range(CH):
                        last = e.tensor_scalar(hot[i][:, j, :], iota[:, :], rel[i][:, j:j + 1], None, ALU.is_equal)
                    last.then_inc(outsem, 1)

                def add_sums(w, outsem):
                    e.tensor_tensor(agg[:, bass.ds(w, 1), :].squeeze(1), ps_g[:, 0:SUMS],
                                    agg[:, bass.ds(w, 1), :].squeeze(1), ALU.add).then_inc(outsem, 1)

                def first(s, n, lo):
                    b = n * SLOTS + s
                    wait(e, first_done, b - 1)
                    compare(s % 2, b, lo, rel_ready, b + 1, hot_ready)

                def finish(s, n, lo, extra):
                    b = n * SLOTS + s
                    with e.If(extra > 0):
                        count = e.snap(further, min_val=1, max_val=1 << 14)
                        compare(2, b, window(nc, e, lo + 1), more_rel, count, more_ready)
                    e.wait_ge(first_done, b + 1)
                    add_sums(lo, g_taken)
                    with e.If(extra > 0):
                        with e.Fori(0, extra) as w:
                            count = e.snap(further, min_val=1, max_val=1 << 14)
                            here = window(nc, e, lo + w + 1)
                            with e.If(w > 0):
                                compare(2, b, here, more_rel, count, more_ready)
                            e.wait_ge(more_done, count)
                            add_sums(here, more_taken)
                            e.reg_add(further, further, 1)
                    e.nop().then_inc(batch_done, 1)

                def products(x, g):
                    whole = x[:, 4 * g:4 * g + 4, :]
                    shifted = AP(whole.tensor, whole.offset, [list(whole.ap[0]), [EXT, 4], [1, 16], [1, HD]])
                    plain = x[:, 4 * g:4 * g + 4, 0:HD].unsqueeze(2).broadcast_to([P, 4, 16, HD])
                    return e.tensor_tensor(quad[g][:, :, :].rearrange("p h (s i) -> p h s i", i=HD), plain, shifted, ALU.mult)

                def tail_products(x):
                    return e.tensor_tensor(tail[:, :, HD:HD + 16], x[:, :, 0:16], x[:, :, 16:32], ALU.mult)

                def more_key_products():
                    products(kext, 1)
                    tail_products(kext).then_inc(feat_ready, 1)

                def keys(turn, u, t, rows):
                    pair, (s1, n1), (s2, n2) = batches_of(turn, u, t, 0)
                    (lo1, more1), (lo2, more2) = windows_of(nc, e, win, pair)
                    first(s1, n1, lo1)
                    if later(t):
                        more_key_products()
                    e.wait_ge(qkv_ps, t + 1)
                    e.tensor_tensor(qk[:, 0:D], ps_xq[:, D:2 * D], bqkv[:, 0:D], ALU.add)
                    e.tensor_tensor(qk[:, D:2 * D], ps_kv[:, 0:D], bqkv[:, D:2 * D], ALU.add)
                    heads = lambda ap: ap.rearrange("p (h c) -> p h c", c=HD)
                    wait(e, keys_done, t - 1)
                    e.tensor_tensor(v1[u][:, :, 1:1 + HD], heads(ps_kv[:, D:2 * D]), heads(bqkv[:, 2 * D:3 * D]),
                                    ALU.add).then_inc(qk_ready, 1)
                    first(s2, n2, lo2)
                    e.wait_ge(sq_ready, t + 1)
                    e.tensor_reduce(norm2[:, :], heads(square[:, :]), X, ALU.add).then_inc(n2_ready, 1)
                    finish(s1, n1, lo1, more1)
                    e.wait_ge(n_ready, t + 1)
                    e.tensor_scalar(normc[:, 0:H], norm[:, 0:H], SCALE, NORM_EPS, ALU.mult, ALU.max)
                    e.tensor_scalar(normc[:, H:2 * H], norm[:, H:2 * H], NORM_EPS, None, ALU.max).then_inc(dve, 1)
                    e.wait_ge(dve, t * 2 + 1)
                    e.reciprocal(inv[:, :], normc[:, :]).then_inc(dve, 1)
                    e.wait_ge(dve, t * 2 + 2)
                    wide = lambda a: inv[:, a:a + H].unsqueeze(2).broadcast_to([P, H, HD])
                    wait(e, lin_ready, t)
                    e.tensor_tensor(kext[:, :, 0:HD], heads(qk[:, D:2 * D]), wide(H), ALU.mult)
                    wait(e, q_out[u], turn * 16)
                    e.scalar_tensor_tensor(out=qext[u][:, :, 0:HD], in0=heads(qk[:, 0:D]), scalar=SCALE,
                                           in1=wide(0), op0=ALU.mult, op1=ALU.mult).then_inc(ext_ready, 1)
                    e.wait_ge(ext2_ready, t + 1)
                    wait(e, keys_done, t)
                    products(kext, 0)
                    finish(s2, n2, lo2, more2)

                def divide(turn, u, t, g):
                    e.wait_ge(nd_ps, t * 2 + (g + 1))
                    e.reciprocal(rden[g][:, :], nd[g][:, P:2 * P]).then_inc(dve, 1)
                    e.wait_ge(dve, t * 2 + (2 * TILES + g + 1))
                    wait(e, ot_out[u], turn * 16)
                    e.tensor_tensor(ot[u][:, g, :], nd[g][:, 0:P], rden[g][:, :], ALU.mult).then_inc(o_ready, 1)

                def query_products(turn, u, t, g):
                    if g == 0:
                        e.wait_ge(qx_in[u], turn * 16 + 16)
                        wait(e, t_ps, t * 10 - 5)
                        products(qext[u], 0).then_inc(qfeat_ready, 1)
                    else:
                        wait(e, t_ps, t * 10)
                        products(qext[u], 1)
                        tail_products(qext[u]).then_inc(qfeat_ready, 1)

                def outputs(turn, u, t, rows):
                    pair, (s1, n1), (s2, n2) = batches_of(turn, u, t, 1)
                    (lo1, more1), (lo2, more2) = windows_of(nc, e, win, pair)
                    first(s1, n1, lo1)
                    if later(t):
                        before_turn, before_u = before(turn, u)
                        divide(before_turn, before_u, t - 1, 1)
                    if rows == P:
                        query_products(turn + u, 1 - u, t + 1, 0)
                    finish(s1, n1, lo1, more1)
                    first(s2, n2, lo2)
                    if rows == P:
                        query_products(turn + u, 1 - u, t + 1, 1)
                    divide(turn, u, t, 0)
                    finish(s2, n2, lo2, more2)

                tile_loop(e, keys)
                more_key_products()
                e.wait_ge(keys_done, TILES)
                for p in range(4):
                    e.tensor_copy(msum[0:97, p, 0:QUAD], bank[p][0:97, :])
                e.tensor_copy(msum[0:97, :, QUAD:QUAD + TAIL],
                              ps_tail[0:97, :].rearrange("p (a b) -> p a b", a=4)[:, :, 0:TAIL]).then_inc(msum_ready, 1)
                query_products(0, 0, 0, 0)
                e.wait_ge(mt_ps, 1)
                for h in range(H):
                    src = bank[h // 2][:, :].rearrange("p (c b) -> p c b", b=P)[:, :, 64 * (h % 2):64 * (h % 2) + 1 + HD]
                    w = weight[:, h, 0:4].unsqueeze(2).broadcast_to([P, 4, HD])
                    e.tensor_tensor(mnum[:, h, 0:4, :], src[:, :, 1:1 + HD], w, ALU.mult)
                    e.tensor_tensor(mden[:, h, 0:4, :], src[:, :, 0:1].broadcast_to([P, 4, HD]), w, ALU.mult)
                for half in range(2):
                    src = ps_tail[0:TAIL, :].rearrange("p (a b) -> p a b", b=P)[:, :, 64 * half:64 * half + 1 + HD]
                    of_half = lambda m: m[0:TAIL, :, 4, :].rearrange("p (a b) c -> p a b c", b=2)[:, :, half, :]
                    w = weight[0:TAIL, :, 4].rearrange("p (a b) -> p a b", b=2)[:, :, half:half + 1].broadcast_to([TAIL, 4, HD])
                    e.tensor_tensor(of_half(mnum), src[:, :, 1:1 + HD], w, ALU.mult)
                    last = e.tensor_tensor(of_half(mden), src[:, :, 0:1].broadcast_to([TAIL, 4, HD]), w, ALU.mult)
                last.then_inc(m_ready, 1)
                query_products(0, 0, 0, 1)
                tile_loop(e, outputs)
                divide(PAIRS, 0, TILES - 1, 1)


def node_stage(nc, A, cst, agg, pos, units, ends, d_xt, d_ot, d_x1, d_slot, node_weights, hold_done,
               expert_weights, w_in):
    B = 4
    with ExitStack() as ctx:
        sb = lambda name, shape, dt: ctx.enter_context(nc.sbuf_tensor(name, shape, dt))
        sem = lambda name: ctx.enter_context(nc.semaphore(name))
        each = lambda name: [sem(f"{name}{u}") for u in range(B)]
        wgnn, wproj, bias, wg, bg = node_weights
        upper = sb("g_upper", [P, P], BF16)
        ones = sb("g_ones", [P, P], BF16)
        zero = sb("g_zero", [P, 2, D], F32)
        eps = sb("g_eps", [P, 1], F32)
        held = sb("g_held", [1, 4], F32)
        taken = sb("g_taken", [P, NX], F32)
        xt = [sb(f"g_xt{u}", [P, 2, P], F32) for u in range(B)]
        ot = [sb(f"g_ot{u}", [P, 2, P], F32) for u in range(B)]
        xr = [sb(f"g_x{u}", [P, D], F32) for u in range(B)]
        biased = [sb(f"g_biased{u}", [P, D], F32) for u in range(2)]
        mixed = [sb(f"g_mixed{u}", [P, D], F32) for u in range(2)]
        deg = sb("g_deg", [P, TILES], F32)
        rdeg = sb("g_rdeg", [P, TILES], F32)
        mean = sb("g_mean", [P, D], F32)
        meant = sb("g_meant", [P, 2, P], F32)
        dump = sb("g_dump", [P, D], F32)
        ss = sb("g_ss", [P, 1], F32)
        norm = sb("g_norm", [P, 1], F32)
        rnorm = sb("g_rnorm", [P, 1], F32)
        x1 = [sb(f"g_x1{u}", [P, D], F32) for u in range(B)]
        stats = sb("g_stats", [P, 6], F32)
        mv = sb("g_mv", [P, 2], F32)
        std = sb("g_std", [P, 1], F32)
        rstd = sb("g_rstd", [P, 1], F32)
        x2 = [sb(f"g_x2{u}", [P, D], F32) for u in range(B)]
        x2t = sb("g_x2t", [P, 2, P], F32)
        score = sb("g_score", [P, NX], F32)
        best = sb("g_best", [P, NX], F32)
        which = sb("g_which", [P, NX], U32)
        whichf = sb("g_whichf", [P, 2], F32)
        chosen = sb("g_chosen", [P, 2, NX], F32)
        mask = sb("g_mask", [P, NX], BF16)
        rank = sb("g_rank", [P, NX], F32)
        slots = sb("g_slots", [P, 2, NX], F32)
        slotf = sb("g_slotf", [P, 2], F32)
        sidx = [sb(f"g_sidx{u}", [P, 2], I32) for u in range(B)]
        cnt = sb("g_cnt", [P, NX], F32)
        cnti = sb("g_cnti", [P, NX], I32)
        unit8 = sb("g_unit8", [P, NX], I32)
        up = sb("g_up", [P, NX], F32)
        posf = sb("g_posf", [P, 2 * TILES], F32)
        rowf = sb("g_rowf", [P, 2 * TILES], F32)
        moved = sb("g_moved", [P, 2 * TILES], F32)
        bank = [ctx.enter_context(nc.psum_tensor(f"g_bank{i}", [P, 512], F32)) for i in range(7)]
        ps_a, ps_b, ps_s, ps_r, ps_p = (*bank[0:4], bank[6])
        ps_o = bank[4:6]

        consts = sem("g_consts")
        rows_in, x1_out = each("g_rows_in"), each("g_x1_out")
        slot_out = each("g_slot_out")
        rdeg_ready, rnorm_ready, rstd_ready = sem("g_rdeg_ready"), sem("g_rnorm_ready"), sem("g_rstd_ready")
        stats_ready, score_ready, which_ready = sem("g_stats_ready"), sem("g_score_ready"), sem("g_which_ready")
        number_ready, bias_ready = sem("g_number_ready"), sem("g_bias_ready")
        odd_zero_out = sem("g_odd_zero_out")
        p_ps, biased_ready, mixed_ready = sem("g_p_ps"), sem("g_biased_ready"), sem("g_mixed_ready")
        mean_ready, a_ps, at_ready, o_ps = sem("g_mean_ready"), sem("g_a_ps"), sem("g_at_ready"), sem("g_o_ps")
        ss_ready, norm_ready, x1_ready = sem("g_ss_ready"), sem("g_norm_ready"), sem("g_x1_ready")
        var_ready, std_ready, x2_ready = sem("g_var_ready"), sem("g_std_ready"), sem("g_x2_ready")
        b_ps, bt_ready, s_ps, mask_ready, r_ps = sem("g_b_ps"), sem("g_bt_ready"), sem("g_s_ps"), sem("g_mask_ready"), sem("g_r_ps")
        slot_ready, tile_done, ends_ready, zero_out = sem("g_slot_ready"), sem("g_tile_done"), sem("g_ends_ready"), sem("g_zero_out")
        best_ready, chosen_ready, rank_ready = sem("g_best_ready"), sem("g_chosen_ready"), sem("g_rank_ready")
        slots_ready, slotf_ready, pos_ready, fin = sem("g_slots_ready"), sem("g_slotf_ready"), sem("g_pos_ready"), sem("g_fin")

        def later(t):
            return not isinstance(t, int) or t > 0

        def turned(ps):
            return ps[:, 0:2 * P].rearrange("p (k r) -> p k r", k=2)

        def zeros(e, first, done):
            e.wait_ge(ends_ready, 1)
            for x in range(first, NX, 2):
                end = e.value_load(ends[0:1, x:x + 1], min_val=x * CAP, max_val=x * CAP + N)
                e.dma_start(d_slot[bass.ds(end, 2 * P), :].rearrange("(j p) c -> p j c", p=P), zero[:, :, :]).then_inc(done, 16)
            e.wait_ge(done, 16 * (NX // 2))

        with nc.Block() as block:

            @block.sync
            def _(e):
                def load(turn, u, t, rows):
                    wait(e, o_ps, t + (1 - B))
                    e.dma_start(xt[u][:, :, :].rearrange("p k r -> p (k r)"), rows_of(d_xt, t, P, D)).then_inc(rows_in[u], 16)
                    wait(e, mixed_ready, t + (1 - B))
                    e.dma_start(ot[u][:, :, :].rearrange("p k r -> p (k r)"), rows_of(d_ot, t, P, D)).then_inc(rows_in[u], 16)
                    e.dma_start(xr[u][:, :], rows_of(A["x"], t, P, D)).then_inc(rows_in[u], 16)

                four_tile_loop(e, load)
                for u in range(2):
                    load_expert(e, A, expert_weights, w_in, u, u)
                zeros(e, 0, zero_out)
                for u in range(2):
                    e.wait_ge(w_in[u], 64)

            @block.gpsimd
            def _(e):
                last_slot = e.alloc_register("last_slot")
                e.reg_mov(last_slot, NX * CAP - 1)

                def add_bias(u, t, count):
                    e.wait_ge(rows_in[u], count)
                    wait(e, mixed_ready, t - 1)
                    e.tensor_tensor(biased[u % 2][:, :], xr[u][:, :], bias[:, 0, :], ALU.add).then_inc(biased_ready, 1)

                def scatter(u, t, rows):
                    e.wait_ge(slot_ready, t + 1)
                    hold(e, hold_done)
                    for k in range(2):
                        e.indirect_dma_start(out=d_slot[:, :], out_offset=bass.IndirectOffsetOnAxis(ap=sidx[u][0:rows, k:k + 1], axis=0),
                                             in_=x2[u][0:rows, :], in_offset=None, bounds_check=last_slot,
                                             oob_is_err=False).then_inc(slot_out[u], 16)

                e.wait_ge(bias_ready, 1)
                add_bias(0, 0, 48)

                def tile(turn, u, t, rows):
                    if rows == P:
                        add_bias((u + 1) % B, t + 1, (turn + (u + 1) // B) * 48 + 48)
                    if later(t):
                        scatter((u - 1) % B, t - 1, P)

                four_tile_loop(e, tile)
                scatter((TILES - 1) % B, TILES - 1, LAST)
                for u in range(B):
                    e.wait_ge(slot_out[u], 32 * len(range(u, TILES, B)))

            @block.tensor
            def _(e):
                e.wait_ge(consts, 1)
                eye = cst[:, C_EYE:C_EYE + P]

                def product(u, t, count):
                    e.wait_ge(rows_in[u], count)
                    wait(e, x1_ready, t - 1)
                    wait(e, mixed_ready, t)
                    for k in range(2):
                        nc.tensor.matmul(ps_o[u % 2][:, 0:D], xt[u][:, k, :], wgnn[:, k, :], start=(k == 0), stop=False)
                    e.wait_ge(mean_ready, t + 1)
                    wait(e, at_ready, t)
                    for k in range(2):
                        last = nc.tensor.transpose(ps_a[:, k * P:(k + 1) * P], mean[:, k * P:(k + 1) * P], eye)
                    last.then_inc(a_ps, 1)
                    for k in range(2):
                        last = nc.tensor.matmul(ps_p[:, 0:D], ot[u][:, k, :], wproj[:, k, :], start=(k == 0), stop=(k == 1))
                    last.then_inc(p_ps, 1)

                def mean_product(u, t):
                    e.wait_ge(at_ready, t + 1)
                    for k in range(2):
                        last = nc.tensor.matmul(ps_o[u % 2][:, 0:D], meant[:, k, :], wgnn[:, 2 + k, :],
                                                start=False, stop=(k == 1))
                    last.then_inc(o_ps, 1)

                def ranks(t, rows):
                    e.wait_ge(mask_ready, t + 1)
                    wait(e, tile_done, t)
                    nc.tensor.matmul(ps_r[0:rows, 0:NX], upper[0:rows, 0:rows], mask[0:rows, :], start=True, stop=True)
                    nc.tensor.matmul(ps_r[:, NX:2 * NX], ones[0:rows, :], mask[0:rows, :], start=True, stop=True,
                                     skip_group_check=True).then_inc(r_ps, 1)

                def tile(turn, u, t, rows):
                    if rows == P:
                        product((u + 1) % B, t + 1, (turn + (u + 1) // B) * 48 + 48)
                        mean_product((u + 1) % B, t + 1)
                    e.wait_ge(x2_ready, t + 1)
                    wait(e, bt_ready, t)
                    for k in range(2):
                        last = nc.tensor.transpose(ps_b[:, k * P:k * P + rows], x2[u][0:rows, k * P:(k + 1) * P],
                                                   cst[0:rows, C_EYE:C_EYE + rows])
                    last.then_inc(b_ps, 1)
                    if later(t):
                        ranks(t - 1, P)
                    e.wait_ge(bt_ready, t + 1)
                    wait(e, score_ready, t)
                    for k in range(2):
                        last = nc.tensor.matmul(ps_s[0:rows, 0:NX], x2t[:, k, 0:rows], wg[:, k, :], start=(k == 0), stop=(k == 1))
                    last.then_inc(s_ps, 1)

                product(0, 0, 48)
                mean_product(0, 0)
                four_tile_loop(e, tile)
                ranks(TILES - 1, LAST)

            @block.scalar
            def _(e):
                e.wait_ge(consts, 1)

                def mean_turned(t):
                    wait(e, a_ps, t)
                    e.activation(mean[:, :], agg[:, bass.ds(t, 1), 0:D].squeeze(1), ACT.Copy,
                                 scale=rdeg[:, bass.ds(t, 1)]).then_inc(mean_ready, 1)
                    e.wait_ge(a_ps, t + 1)
                    e.activation(meant[:, :, :], turned(ps_a), ACT.Copy).then_inc(at_ready, 1)

                def output_norm(u, t):
                    e.wait_ge(o_ps, t + 1)
                    e.activation(dump[:, :], ps_o[u % 2][:, 0:D], ACT.Square, accum_out=ss[:, 0:1]).then_inc(ss_ready, 1)
                    e.wait_ge(ss_ready, t + 1)
                    wait(e, rnorm_ready, t)
                    e.activation(norm[:, :], ss[:, :], ACT.Sqrt).then_inc(norm_ready, 1)

                def tile(turn, u, t, rows):
                    if rows == P:
                        mean_turned(t + 1)
                    e.wait_ge(var_ready, t + 1)
                    e.activation(std[0:rows, :], mv[0:rows, 1:2], ACT.Sqrt, bias=eps[0:rows, 0:1]).then_inc(std_ready, 1)
                    e.dma_start(rows_of(d_x1, t, P, D), x1[u][:, :]).then_inc(x1_out[u], 16)
                    e.wait_ge(b_ps, t + 1)
                    wait(e, s_ps, t)
                    e.activation(x2t[:, :, 0:rows], turned(ps_b)[:, :, 0:rows], ACT.Copy).then_inc(bt_ready, 1)
                    if rows == P:
                        output_norm((u + 1) % B, t + 1)

                e.wait_ge(rdeg_ready, 1)
                mean_turned(0)
                output_norm(0, 0)
                four_tile_loop(e, tile)
                for u in range(B):
                    e.wait_ge(x1_out[u], 16 * len(range(u, TILES, B)))
                zeros(e, 1, odd_zero_out)

            @block.vector
            def _(e):
                e.tensor_copy(upper[:, :], cst[:, C_UP:C_UP + P])
                e.tensor_copy(taken[:, :], cst[:, C_BASE:C_BASE + NX])
                e.memset(ones[:, :], 1.0)
                e.memset(zero[:, :, :], 0.0)
                e.memset(eps[:, :], LN_EPS)
                e.memset(pos[:, :, :], 0)
                for u in range(B):
                    e.memset(x1[u][:, :], 0.0)
                e.tensor_scalar(deg[:, :], agg[:, :, D], 1.0, None, ALU.max)
                e.drain().then_inc(consts, 1)
                e.wait_ge(consts, 1)
                e.reciprocal(rdeg[:, :], deg[:, :]).then_inc(rdeg_ready, 1)
                e.wait_ge(rdeg_ready, 1)

                def own(i, sem, value):
                    e.wait_ge(sem, value)
                    e.memset(held[:, i:i + 1], 0.0)

                def residual(u, t):
                    e.wait_ge(p_ps, t + 1)
                    e.wait_ge(biased_ready, t + 1)
                    wait(e, x1_ready, t - 1)
                    e.tensor_tensor(mixed[u % 2][:, :], ps_p[:, 0:D], biased[u % 2][:, :], ALU.add).then_inc(mixed_ready, 1)

                def scores(t, rows):
                    e.wait_ge(s_ps, t + 1)
                    e.tensor_tensor(score[0:rows, :], ps_s[0:rows, 0:NX], bg[0:rows, :], ALU.add).then_inc(score_ready, 1)

                def best_scores(t, rows):
                    own(0, score_ready, t + 1)
                    e.max(best[0:rows, :], score[0:rows, :]).then_inc(best_ready, 1)

                def best_experts(t, rows):
                    own(1, best_ready, t + 1)
                    e.max_index(which[0:rows, :], best[0:rows, :], score[0:rows, :]).then_inc(which_ready, 1)

                def expert_numbers(t, rows):
                    e.wait_ge(which_ready, t + 1)
                    e.tensor_copy(whichf[0:rows, :], which[0:rows, 0:2]).then_inc(number_ready, 1)

                def masks(t, rows):
                    e.wait_ge(number_ready, t + 1)
                    for k in range(2):
                        last = e.tensor_scalar(chosen[0:rows, k, :], cst[0:rows, C_E:C_E + NX], whichf[0:rows, k:k + 1],
                                               None, ALU.is_equal)
                    last.then_inc(chosen_ready, 1)
                    e.wait_ge(chosen_ready, t + 1)
                    e.tensor_tensor(mask[0:rows, :], chosen[0:rows, 0, :], chosen[0:rows, 1, :], ALU.add).then_inc(mask_ready, 1)

                def ranks(t, rows):
                    e.wait_ge(r_ps, t + 1)
                    e.tensor_tensor(rank[0:rows, :], ps_r[0:rows, 0:NX], taken[0:rows, :], ALU.add).then_inc(rank_ready, 1)
                    e.wait_ge(rank_ready, t + 1)
                    e.tensor_tensor(taken[:, :], ps_r[:, NX:2 * NX], taken[:, :], ALU.add).then_inc(tile_done, 1)
                    e.tensor_tensor(slots[0:rows, :, :], chosen[0:rows, :, :], rank[0:rows, :].unsqueeze(1).broadcast_to([rows, 2, NX]),
                                    ALU.mult).then_inc(slots_ready, 1)

                def slot_numbers(u, t, rows):
                    e.wait_ge(slots_ready, t + 1)
                    e.tensor_reduce(slotf[0:rows, :], slots[0:rows, :, :], X, ALU.add).then_inc(slotf_ready, 1)
                    e.wait_ge(slotf_ready, t + 1)
                    e.tensor_copy(sidx[u][0:rows, :], slotf[0:rows, :]).then_inc(slot_ready, 1)
                    e.tensor_copy(pos[0:rows, bass.ds(t, 1), :].squeeze(1), slotf[0:rows, :]).then_inc(pos_ready, 1)
                    e.wait_ge(tile_done, t + 1)

                def tile(turn, u, t, rows):
                    gate = later(t)
                    e.wait_ge(norm_ready, t + 1)
                    e.reciprocal(rnorm[0:rows, :], norm[0:rows, :]).then_inc(rnorm_ready, 1)
                    if gate:
                        scores(t - 1, P)
                    e.wait_ge(rnorm_ready, t + 1)
                    e.wait_ge(mixed_ready, t + 1)
                    wait(e, x1_out[u], turn * 16)
                    e.scalar_tensor_tensor(out=x1[u][0:rows, :], in0=ps_o[u % 2][0:rows, 0:D], scalar=rnorm[0:rows, 0:1],
                                           in1=mixed[u % 2][0:rows, :], op0=ALU.mult, op1=ALU.add).then_inc(x1_ready, 1)
                    if gate:
                        best_scores(t - 1, P)
                    own(2, x1_ready, t + 1)
                    e.bn_stats(stats[0:rows, :], x1[u][0:rows, :]).then_inc(stats_ready, 1)
                    if gate:
                        best_experts(t - 1, P)
                    own(3, stats_ready, t + 1)
                    e.bn_aggr(mv[0:rows, :], stats[0:rows, :]).then_inc(var_ready, 1)
                    if gate:
                        expert_numbers(t - 1, P)
                        masks(t - 1, P)
                    e.wait_ge(std_ready, t + 1)
                    e.reciprocal(rstd[0:rows, :], std[0:rows, :]).then_inc(rstd_ready, 1)
                    e.wait_ge(rstd_ready, t + 1)
                    wait(e, slot_out[u], turn * 32)
                    e.tensor_scalar(x2[u][0:rows, :], x1[u][0:rows, :], mv[0:rows, 0:1], rstd[0:rows, 0:1],
                                    ALU.subtract, ALU.mult).then_inc(x2_ready, 1)
                    if rows == P:
                        residual((u + 1) % B, t + 1)
                    if gate:
                        ranks(t - 1, P)
                        slot_numbers((u - 1) % B, t - 1, P)

                e.tensor_tensor(bias[:, 0, :], bias[:, 0, :], bias[:, 1, :], ALU.add).then_inc(bias_ready, 1)
                residual(0, 0)
                four_tile_loop(e, tile)
                t = TILES - 1
                scores(t, LAST)
                best_scores(t, LAST)
                best_experts(t, LAST)
                expert_numbers(t, LAST)
                masks(t, LAST)
                ranks(t, LAST)
                slot_numbers(t % B, t, LAST)
                e.wait_ge(pos_ready, TILES)
                e.tensor_copy(ends[:, :], taken[0:1, :]).then_inc(ends_ready, 1)
                e.tensor_tensor(cnt[:, :], taken[:, :], cst[:, C_BASE:C_BASE + NX], ALU.subtract)
                e.tensor_copy(posf[:, :], pos[:, 0:TILES, :].rearrange("p t k -> p (t k)")).then_inc(fin, 1)
                e.wait_ge(fin, 1)
                e.tensor_scalar(cnti[:, :], cnt[:, :], UNIT - 1.0, float(UNIT), ALU.add, ALU.max).then_inc(fin, 1)
                e.wait_ge(fin, 2)
                e.tensor_scalar(unit8[:, :], cnti[:, :], 8, None, ALU.arith_shift_right).then_inc(fin, 1)
                e.wait_ge(fin, 3)
                e.tensor_copy(units[:, :], unit8[0:1, :])
                e.tensor_scalar(up[:, :], unit8[:, :], -float(UNIT), float(CAP), ALU.mult, ALU.add)
                e.tensor_copy(rowf[:, :], posf[:, :]).then_inc(fin, 1)
                e.wait_ge(fin, 4)
                for x in range(1, NX):
                    e.tensor_scalar(moved[:, :], posf[:, :], float(x * CAP), up[:, x - 1:x], ALU.is_ge, ALU.mult).then_inc(fin, 1)
                    e.wait_ge(fin, 3 + 2 * x)
                    e.tensor_tensor(rowf[:, :], rowf[:, :], moved[:, :], ALU.subtract).then_inc(fin, 1)
                    e.wait_ge(fin, 4 + 2 * x)
                e.tensor_copy(pos[:, 0:TILES, :].rearrange("p t k -> p (t k)"), rowf[:, :])
                e.drain().then_inc(fin, 1)


def load_expert(e, A, buffers, w_in, u, x):
    w1, w2, b1, b2 = buffers
    e.dma_start(w1[u][:, :, :], A["w1"][bass.ds(x, 1), :, :].rearrange("o (k p) f -> p (o k) f", p=P)).then_inc(w_in[u], 16)
    e.dma_start(w2[u][:, :, :], A["w2"][bass.ds(x, 1), :, :].rearrange("o (k p) f -> p (o k) f", p=P)).then_inc(w_in[u], 16)
    e.dma_start(b1[u][:, :], A["b1"][bass.ds(x, 1), :, :].rearrange("o p k -> (o p) k")).then_inc(w_in[u], 16)
    e.dma_start(b2[u][:, :], A["b2"][bass.ds(x, 1), :].squeeze(0).partition_broadcast(P)).then_inc(w_in[u], 16)


def expert_stage(nc, A, cst, units, d_slot, d_y, expert_weights, w_in):
    U = UNIT
    KF = FF // P
    with ExitStack() as ctx:
        sb = lambda name, shape, dt: ctx.enter_context(nc.sbuf_tensor(name, shape, dt))
        sem = lambda name: ctx.enter_context(nc.semaphore(name))
        two = lambda name: [sem(f"{name}{u}") for u in range(2)]
        w1, w2, b1, b2 = expert_weights
        x = sb("e_x", [P, 2, D], F32)
        zero = sb("e_zero", [P, 2, D], F32)
        xt = sb("e_xt", [P, 2, U], F32)
        ht = sb("e_ht", [P, KF, U], F32)
        y = sb("e_y", [P, 2, D], F32)
        ps_x = ctx.enter_context(nc.psum_tensor("e_psx", [P, 2, U], F32))
        ps_h = [ctx.enter_context(nc.psum_tensor(f"e_psh{i}", [P, 512], F32)) for i in range(KF)]
        ps_y = [ctx.enter_context(nc.psum_tensor(f"e_psy{i}", [P, 512], F32)) for i in range(2)]
        x_in, y_out = sem("e_x_in"), sem("e_y_out")
        x_ps, xt_ready, h_ps, h_ready, y_ps, y_ready, y_free = (
            sem("e_x_ps"), sem("e_xt_ready"), sem("e_h_ps"), sem("e_h_ready"), sem("e_y_ps"), sem("e_y_ready"), sem("e_y_free"))
        expert_done, zero_ready, zero_out = sem("e_expert_done"), sem("e_zero_ready"), sem("e_zero_out")

        def experts(e, body, first=0):
            with e.Fori(first, NX // 2) as pair:
                for u in range(2):
                    body(pair, u, pair * 2 + u)

        def unit_loop(e, x, body):
            count = e.value_load(units[0:1, bass.ds(x, 1)], min_val=1, max_val=-(-N // U))
            with e.Fori(0, count) as i:
                body(i)

        class Turn:

            def __init__(self, e, name):
                self.e, self.reg = e, e.alloc_register(name)
                e.reg_mov(self.reg, 1)

            def now(self):
                return self.e.snap(self.reg, min_val=1, max_val=UNITS)

            def next(self):
                self.e.reg_add(self.reg, self.reg, 1)

        with nc.Block() as block:

            @block.sync
            def _(e):
                turn = Turn(e, "sp_unit")

                def expert(pair, u, x_):
                    if not isinstance(pair, int):
                        e.wait_ge(expert_done, x_ + 1)
                        load_expert(e, A, expert_weights, w_in, u, x_)

                    def unit(i):
                        n = turn.now()
                        e.wait_ge(x_ps, n)
                        e.dma_start(x[:, :, :], d_slot[bass.ds(x_ * CAP + i * U, U), :].rearrange("(j p) c -> p j c", p=P)).then_inc(x_in, 16)
                        turn.next()

                    unit_loop(e, x_, unit)

                for u in range(2):
                    expert(0, u, u)
                experts(e, expert, 1)
                e.wait_ge(x_ps, turn.now())
                e.dma_start(x[:, :, :], d_slot[0:U, :].rearrange("(j p) c -> p j c", p=P)).then_inc(x_in, 16)

            @block.gpsimd
            def _(e):
                turn = Turn(e, "pool_unit")
                e.memset(zero[:, :, :], 0.0).then_inc(zero_ready, 1)
                e.nop().then_inc(y_free, 1)
                total = e.value_load(units[0:1, 0:1], min_val=1, max_val=-(-N // U))
                for x in range(1, NX):
                    total = total + e.value_load(units[0:1, x:x + 1], min_val=1, max_val=-(-N // U))
                total = nc.s_assert_within(e.snap(total), NX, UNITS - 1, skip_runtime_bounds_check_because=
                                           "the experts have 2 N rows, and less than a unit more each")
                zeros = Turn(e, "pool_zeros")
                e.wait_ge(zero_ready, 1)
                with e.Fori(total, UNITS) as n:
                    e.dma_start(d_y[bass.ds(n * U, U), :].rearrange("(j p) c -> p j c", p=P), zero[:, :, :]).then_inc(zero_out, 16)
                    e.wait_ge(zero_out, zeros.now() * 16)
                    zeros.next()

                def expert(pair, u, x_):
                    def unit(i):
                        n = turn.now()
                        e.wait_ge(y_ready, n + 1)
                        e.dma_start(d_y[bass.ds((n - 1) * U, U), :].rearrange("(j p) c -> p j c", p=P), y[:, :, :]).then_inc(y_out, 16)
                        e.wait_ge(y_out, n * 16)
                        e.nop().then_inc(y_free, 1)
                        turn.next()

                    unit_loop(e, x_, unit)

                experts(e, expert)

            @block.tensor
            def _(e):
                turn = Turn(e, "pe_unit")
                e.nop().then_inc(x_ps, 1)
                e.nop().then_inc(expert_done, 2)

                def rows_turned(n):
                    e.wait_ge(x_in, n * 16)
                    e.wait_ge(xt_ready, n)
                    for k in range(2):
                        for j in range(2):
                            last = nc.tensor.transpose(ps_x[:, k, j * P:(j + 1) * P], x[:, j, k * P:(k + 1) * P],
                                                       cst[:, C_EYE:C_EYE + P])
                    last.then_inc(x_ps, 1)

                def expert(pair, v, x_):
                    e.wait_ge(w_in[v], pair * 64 + 64)

                    def unit(i):
                        n = turn.now()
                        e.wait_ge(xt_ready, n + 1)
                        e.wait_ge(h_ready, n * KF - (KF - 1))
                        for c in range(KF):
                            for k in range(2):
                                last = nc.tensor.matmul(ps_h[c][:, 0:U], w1[v][:, k, c * P:(c + 1) * P], xt[:, k, :],
                                                        start=(k == 0), stop=(k == 1))
                            last.then_inc(h_ps, 1)
                        rows_turned(n + 1)
                        e.wait_ge(y_ready, n)
                        for c in range(KF):
                            e.wait_ge(h_ready, n * KF + (c + 2 - KF))
                            for j in range(2):
                                last = nc.tensor.matmul(ps_y[j][:, 0:D], ht[:, c, j * P:(j + 1) * P], w2[v][:, c, :],
                                                        start=(c == 0), stop=(c == KF - 1), skip_group_check=True)
                        last.then_inc(y_ps, 1)
                        turn.next()

                    unit_loop(e, x_, unit)

                rows_turned(turn.now())
                experts(e, expert)

            @block.scalar
            def _(e):
                turn = Turn(e, "act_unit")
                e.nop().then_inc(h_ready, 1)

                def expert(pair, v, x_):
                    e.wait_ge(w_in[v], pair * 64 + 64)

                    def unit(i):
                        n = turn.now()
                        e.wait_ge(y_ps, n)
                        for c in range(KF):
                            e.wait_ge(h_ps, n * KF + (c + 1 - KF))
                            e.activation(ht[:, c, :], ps_h[c][:, 0:U], ACT.Gelu, bias=b1[v][:, c:c + 1]).then_inc(h_ready, 1)
                        turn.next()

                    unit_loop(e, x_, unit)

                experts(e, expert)

            @block.vector
            def _(e):
                turn = Turn(e, "dve_unit")
                e.nop().then_inc(xt_ready, 1)
                e.nop().then_inc(y_ready, 1)
                e.nop().then_inc(y_ps, 1)

                def copy_rows(n):
                    e.wait_ge(x_ps, n + 1)
                    e.tensor_copy(xt[:, :, :], ps_x[:, :, :]).then_inc(xt_ready, 1)

                def expert(pair, v, x_):
                    e.wait_ge(w_in[v], pair * 64 + 64)

                    def unit(i):
                        n = turn.now()
                        copy_rows(n + 1)
                        e.wait_ge(y_free, n)
                        e.wait_ge(y_ps, n + 1)
                        for j in range(2):
                            last = e.tensor_tensor(y[:, j, :], ps_y[j][:, 0:D], b2[v][:, :], ALU.add)
                        last.then_inc(y_ready, 1)
                        turn.next()

                    unit_loop(e, x_, unit)
                    e.wait_ge(y_ready, turn.now())
                    e.nop().then_inc(expert_done, 1)

                copy_rows(turn.now())
                experts(e, expert)


def combine_stage(nc, A, pos, d_x1, d_y, hold_done):
    B = 4
    with ExitStack() as ctx:
        sb = lambda name, shape, dt: ctx.enter_context(nc.sbuf_tensor(name, shape, dt))
        sem = lambda name: ctx.enter_context(nc.semaphore(name))
        each = lambda name: [sem(f"{name}{u}") for u in range(B)]
        idx = [sb(f"c_idx{u}", [P, 2], I32) for u in range(B)]
        x1 = [sb(f"c_x1{u}", [P, D], F32) for u in range(B)]
        ya = [sb(f"c_ya{u}", [P, D], F32) for u in range(B)]
        yb = [sb(f"c_yb{u}", [P, D], F32) for u in range(B)]
        part = [sb(f"c_part{u}", [P, D], F32) for u in range(B)]
        out = [sb(f"c_out{u}", [P, D], F32) for u in range(2)]
        x_in, y_in = each("c_x_in"), each("c_y_in")
        out_done = [sem(f"c_out_done{u}") for u in range(2)]
        idx_ready, part_ready, added = sem("c_idx_ready"), sem("c_part_ready"), sem("c_added")

        with nc.Block() as block:

            @block.sync
            def _(e):
                def load(turn, u, t, rows):
                    wait(e, part_ready, t + (1 - B))
                    e.dma_start(x1[u][:, :], rows_of(d_x1, t, P, D)).then_inc(x_in[u], 16)

                four_tile_loop(e, load)

            @block.gpsimd
            def _(e):
                last_slot = e.alloc_register("last_slot2")
                e.reg_mov(last_slot, UNITS * UNIT - 1)

                def gather(turn, u, t, rows):
                    e.wait_ge(idx_ready, t + 1)
                    wait(e, added, t + (1 - B))
                    hold(e, hold_done)
                    for k, y in ((0, ya), (1, yb)):
                        e.indirect_dma_start(out=y[u][0:rows, :], out_offset=None, in_=d_y[:, :],
                                             in_offset=bass.IndirectOffsetOnAxis(ap=idx[u][0:rows, k:k + 1], axis=0),
                                             bounds_check=last_slot, oob_is_err=False).then_inc(y_in[u], 16)

                four_tile_loop(e, gather)

            @block.scalar
            def _(e):
                def store(turn, u, t, rows):
                    e.wait_ge(added, t + 1)
                    e.dma_start(rows_of(A["out"], t, rows, D), out[u % 2][0:rows, :]).then_inc(out_done[u % 2], 16)

                four_tile_loop(e, store)
                for u in range(2):
                    e.wait_ge(out_done[u], 16 * len(range(u, TILES, 2)))

            @block.vector
            def _(e):
                def index(turn, u, t):
                    wait(e, y_in[u], turn * 32)
                    e.tensor_copy(idx[u][:, :], pos[:, bass.ds(t, 1), :].squeeze(1)).then_inc(idx_ready, 1)

                def add(turn, u, t, rows):
                    e.wait_ge(x_in[u], turn * 16 + 16)
                    e.wait_ge(y_in[u], turn * 32 + 32)
                    e.tensor_tensor(part[u][0:rows, :], x1[u][0:rows, :], ya[u][0:rows, :], ALU.add).then_inc(part_ready, 1)
                    e.wait_ge(part_ready, t + 1)
                    wait(e, out_done[u % 2], turn * 32 + 16 * (u // 2))
                    e.tensor_tensor(out[u % 2][0:rows, :], part[u][0:rows, :], yb[u][0:rows, :], ALU.add).then_inc(added, 1)
                    if not isinstance(t, int) or t + B < TILES:
                        index(turn + 1, u, t + B)

                for u in range(B):
                    index(0, u, u)
                four_tile_loop(e, add)


def kernel(x, src, dst, L0_gnn_weight, L0_gnn_bias, L0_mix_Wqkv, L0_mix_bqkv, L0_mix_Wproj, L0_mix_bproj,
           L0_mix_temperature, L0_ffn_Wg, L0_ffn_bg, L0_ffn_W1, L0_ffn_b1, L0_ffn_W2, L0_ffn_b2):
    import concourse.bacc as bacc
    from concourse.bass_utils import run_bass_kernel_spmd

    x = np.asarray(x)
    src, dst = np.asarray(src), np.asarray(dst)
    pad = BATCHES * CH * P - E
    src = np.concatenate([src, np.full(pad, N, src.dtype)])
    dst = np.concatenate([dst, dst[-pad:]])
    cols = lambda a: np.ascontiguousarray(a.reshape(BATCHES, CH, P).transpose(2, 0, 1).reshape(P, BATCHES * CH))
    arrays = {
        "x": np.concatenate([x, np.zeros((TILES * P - N, D), x.dtype)]),
        "src_cols": cols(src), "dst_cols": cols(dst), "dst_rows": dst.reshape(BATCHES // 2, 2 * CH * P),
        "cst": constants(),
        "wgnn": L0_gnn_weight, "gbias": L0_gnn_bias,
        "wqkv": np.asarray(L0_mix_Wqkv).T, "bqkv": L0_mix_bqkv,
        "wproj": np.asarray(L0_mix_Wproj).T, "bproj": L0_mix_bproj,
        "temp": np.asarray(L0_mix_temperature).reshape(H),
        "wg": L0_ffn_Wg, "bg": L0_ffn_bg,
        "w1": L0_ffn_W1, "b1": np.asarray(L0_ffn_b1).reshape(NX, FF // P, P).transpose(0, 2, 1), "w2": L0_ffn_W2, "b2": L0_ffn_b2,
    }
    arrays = {f"in_{k}": np.ascontiguousarray(a) for k, a in arrays.items()}
    nc = bacc.Bacc("TRN2", target_bir_lowering=False, num_devices=1)
    A = {k[3:]: nc.dram_tensor(k, a.shape, mybir.dt.from_np(a.dtype), kind="ExternalInput").ap() for k, a in arrays.items()}
    A["out"] = nc.dram_tensor("out", (N, D), F32, kind="ExternalOutput").ap()
    build(nc, A)
    r = run_bass_kernel_spmd(nc, [arrays], core_ids=[0])
    return r.results[0]["out"]
```
